# Optimizing a Trainium2 kernel written in Bass

```python
import numpy as np
import jax
import jax.numpy as jnp

def _softmax(x, axis=-1):
    return jax.nn.softmax(x, axis=axis)

def _gelu(x):
    return jax.nn.gelu(x, approximate=True)

def _silu(x):
    return jax.nn.silu(x)

def _sigmoid(x):
    return jax.nn.sigmoid(x)

def _layernorm(x, axis=-1, eps=1e-05):
    m = jnp.mean(x, axis=axis, keepdims=True)
    v = jnp.var(x, axis=axis, keepdims=True)
    return (x - m) / jnp.sqrt(v + eps)

def _scatter_add(tgt, idx, src, axis=0):
    return tgt.at[idx].add(src)

def _segment_sum(src, seg, n):
    return jax.ops.segment_sum(src, seg, n)
kernel_name = 'mk_prb_d1_jaxref_r8_ecc7ff'

def setup_inputs(seed: int=0):
    np.random.seed(seed)
    _w = jnp.asarray

    def _L0_attn_setup():
        import jax, jax.numpy as jnp
        import numpy as np
        D_MODEL = 256
        N_HEADS = 16
        N_KV = 4
        GROUP = N_HEADS // N_KV
        D_K = D_MODEL // N_HEADS
        D_V = D_MODEL // N_KV
        THETA = 10000.0
        Q_DIM = N_HEADS * D_K
        K_DIM = N_KV * D_K
        V_DIM = N_KV * D_V

        def _apply_rope(t, sin, cos):
            half = t.shape[-1] // 2
            x1, x2 = (t[..., :half], t[..., half:])
            rot = jnp.concatenate([-x2, x1], axis=-1)
            return t * cos + rot * sin
        key = jax.random.key(seed)
        k1, k2, k3 = jax.random.split(key, 3)
        x = jax.random.normal(k1, (2, 256, D_MODEL), dtype=jnp.float32)
        W_attn = jax.random.normal(k2, (D_MODEL, Q_DIM + K_DIM + V_DIM), dtype=jnp.float32) * 0.02
        W_out = jax.random.normal(k3, (N_HEADS * D_V, D_MODEL), dtype=jnp.float32) * 0.02
        b_out = jnp.zeros((D_MODEL,), dtype=jnp.float32)
        return {'x': x, 'W_attn': W_attn, 'W_out': W_out, 'b_out': b_out}
    _L0_attn_in = _L0_attn_setup()

    def _L0_ffn_setup():
        import jax, jax.numpy as jnp
        import numpy as np
        H, I, E, K = (256, 512, 8, 2)
        B, S = (1, 256)

        def _silu_mul(gu):
            d = gu.shape[-1] // 2
            return jax.nn.silu(gu[..., :d]) * gu[..., d:]
        key = jax.random.key(seed)
        ks = jax.random.split(key, 6)
        w_scale = 0.02
        return {'x': jax.random.normal(ks[0], (B, S, H), jnp.float32), 'gate_w': jax.random.normal(ks[1], (H, E), jnp.float32) * w_scale, 'base_gate_up': jax.random.normal(ks[2], (H, 2 * I), jnp.float32) * w_scale, 'base_down': jax.random.normal(ks[3], (I, H), jnp.float32) * w_scale, 'expert_gate_up': jax.random.normal(ks[4], (E, H, 2 * I), jnp.float32) * w_scale, 'expert_down': jax.random.normal(ks[5], (E, I, H), jnp.float32) * w_scale}
    _L0_ffn_in = _L0_ffn_setup()
    _d = {'L0_attn_x': _L0_attn_in['x'], 'L0_attn_W_attn': _L0_attn_in['W_attn'], 'L0_attn_W_out': _L0_attn_in['W_out'], 'L0_attn_b_out': _L0_attn_in['b_out'], 'L0_ffn_gate_w': _L0_ffn_in['gate_w'], 'L0_ffn_base_gate_up': _L0_ffn_in['base_gate_up'], 'L0_ffn_base_down': _L0_ffn_in['base_down'], 'L0_ffn_expert_gate_up': _L0_ffn_in['expert_gate_up'], 'L0_ffn_expert_down': _L0_ffn_in['expert_down']}
    _x0 = _d['L0_attn_x']
    _d['L0_attn_x'] = jax.random.normal(jax.random.fold_in(jax.random.key(seed), 1), (2, 1024, 256), dtype=_x0.dtype)
    del _x0
    return _d

def reference(L0_attn_x, L0_attn_W_attn, L0_attn_W_out, L0_attn_b_out, L0_ffn_gate_w, L0_ffn_base_gate_up, L0_ffn_base_down, L0_ffn_expert_gate_up, L0_ffn_expert_down):

    def _L0_attn_ref(x, W_attn, W_out, b_out):
        import jax, jax.numpy as jnp
        import numpy as np
        D_MODEL = 256
        N_HEADS = 16
        N_KV = 4
        GROUP = N_HEADS // N_KV
        D_K = D_MODEL // N_HEADS
        D_V = D_MODEL // N_KV
        THETA = 10000.0
        Q_DIM = N_HEADS * D_K
        K_DIM = N_KV * D_K
        V_DIM = N_KV * D_V

        def _apply_rope(t, sin, cos):
            half = t.shape[-1] // 2
            x1, x2 = (t[..., :half], t[..., half:])
            rot = jnp.concatenate([-x2, x1], axis=-1)
            return t * cos + rot * sin
        B, L, _ = x.shape
        qkv = x @ W_attn
        q = qkv[..., :Q_DIM].reshape(B, L, N_HEADS, D_K).transpose(0, 2, 1, 3)
        k = qkv[..., Q_DIM:Q_DIM + K_DIM].reshape(B, L, N_KV, D_K).transpose(0, 2, 1, 3)
        v = qkv[..., Q_DIM + K_DIM:].reshape(B, L, N_KV, D_V).transpose(0, 2, 1, 3)
        inv_freq = 1.0 / THETA ** (jnp.arange(0, D_K, 2, dtype=jnp.float32) / D_K)
        freqs = jnp.arange(L, dtype=jnp.float32)[:, None] * inv_freq[None, :]
        ang = jnp.concatenate([freqs, freqs], axis=-1)
        sin, cos = (jnp.sin(ang), jnp.cos(ang))
        q = _apply_rope(q.astype(jnp.float32), sin, cos).astype(x.dtype)
        k = _apply_rope(k.astype(jnp.float32), sin, cos).astype(x.dtype)
        qg = q.reshape(B, N_KV, GROUP, L, D_K)
        scores = jnp.einsum('bkgqd,bkld->bkgql', qg, k) / D_K ** 0.5
        probs = jax.nn.softmax(scores, axis=-1)
        ctx = jnp.einsum('bkgql,bkle->bkgqe', probs, v)
        ctx = ctx.reshape(B, N_HEADS, L, D_V).transpose(0, 2, 1, 3).reshape(B, L, N_HEADS * D_V)
        return ctx @ W_out + b_out

    def _L0_ffn_ref(x, gate_w, base_gate_up, base_down, expert_gate_up, expert_down):
        import jax, jax.numpy as jnp
        import numpy as np
        H, I, E, K = (256, 512, 8, 2)
        B, S = (1, 256)

        def _silu_mul(gu):
            d = gu.shape[-1] // 2
            return jax.nn.silu(gu[..., :d]) * gu[..., d:]
        base_y = _silu_mul(x @ base_gate_up) @ base_down
        b, s, h = x.shape
        xf = x.reshape(-1, h)
        n = xf.shape[0]
        n_exp = gate_w.shape[1]
        probs = jax.nn.softmax((xf @ gate_w).astype(jnp.float32), axis=-1)
        w, idx = jax.lax.top_k(probs, K)
        w = (w / w.sum(axis=-1, keepdims=True)).astype(x.dtype)
        comb = jnp.zeros((n, n_exp), x.dtype).at[jnp.arange(n)[:, None], idx].add(w)
        out = jnp.zeros_like(xf)
        for e in range(n_exp):
            y = _silu_mul(xf @ expert_gate_up[e]) @ expert_down[e]
            out = out + comb[:, e:e + 1] * y
        return out.reshape(b, s, h) + base_y
    x = L0_attn_x
    xn = _layernorm(x, axis=-1)
    x = x + _L0_attn_ref(xn, L0_attn_W_attn, L0_attn_W_out, L0_attn_b_out) + _L0_ffn_ref(xn, L0_ffn_gate_w, L0_ffn_base_gate_up, L0_ffn_base_down, L0_ffn_expert_gate_up, L0_ffn_expert_down)
    return x

_drawn_inputs = setup_inputs


def setup_inputs(seed=0):
    import zlib

    import numpy as np

    out = dict(_drawn_inputs(seed))
    spreads = {'L0_attn_b_out': (0.0, 0.789)}
    factors = {'L0_attn_W_attn': 8.0,
     'L0_attn_W_out': 8.0,
     'L0_ffn_gate_w': 3.873,
     'L0_ffn_expert_gate_up': 3.336,
     'L0_ffn_expert_down': 3.34,
     'L0_ffn_base_gate_up': 8.0,
     'L0_ffn_base_down': 8.0}
    for name, (base, spread) in spreads.items():
        noise = np.random.default_rng([zlib.crc32(name.encode()), seed]).standard_normal(out[name].shape)
        drawn = base * np.exp(spread * noise) if base else spread * noise
        out[name] = jnp.asarray(drawn.astype(out[name].dtype))
    for name, factor in factors.items():
        out[name] = (out[name] * factor).astype(out[name].dtype)
    return out
```

```python
from contextlib import ExitStack

import concourse.bass as bass
import concourse.mybir as mybir

P = 128
B, L, D = 2, 1024, 256
NH, NKV, DK, DV = 16, 4, 16, 64
E, I = 8, 512
TOK = B * L
NT = TOK // P
TB = L // P
KC = D // P
IC = I // P
NHK = NH + NKV
QK_COLS = NHK * DK
VG_COLS = NKV * DV + E
XTILES = 2 * NT + E
NF = NT + XTILES
ROWS = NF * P
ST = 64
MCOL = 48
PAIRS = NH // 2
GROUPS = B * NKV
QH = 512
QT = QH // P
UNITS = GROUPS * 2 * (L // QH)
EPS = 1e-5
SCALE = DK ** -0.5

C_ID, C_TRI, C_COS, C_SIN = 0, 128, 256, 384
C_TIE = 512
C_THR = C_TIE + E * E
C_TIX = C_THR + NT
C_ALL = C_TIX + XTILES


def build(nc, x, w_attn, w_out, b_out, gate_w, base_gu, base_dn, exp_gu, exp_dn, consts, out):
    F32, F32R, I32 = mybir.dt.float32, mybir.dt.float32r, mybir.dt.int32
    ALU, ACT, AX = mybir.AluOpType, mybir.ActivationFunctionType, mybir.AxisListType
    ds = bass.ds
    ctx = ExitStack()
    with ctx:
        def sb(name, shape, dt=F32):
            return ctx.enter_context(nc.sbuf_tensor(name, shape, dt))

        def sem(name):
            return ctx.enter_context(nc.semaphore(name))

        xd = nc.dram_tensor("xd", (ROWS, D), F32, kind="Internal").ap()
        yd = nc.dram_tensor("yd", (ROWS, D), F32, kind="Internal").ap()
        qd = nc.dram_tensor("qd", ((GROUPS + 1) * 2 * L, P), F32, kind="Internal").ap()
        kd = nc.dram_tensor("kd", ((GROUPS + 2) * L, ST), F32, kind="Internal").ap()
        vd = nc.dram_tensor("vd", ((GROUPS + 1) * L, DV), F32, kind="Internal").ap()
        cd = nc.dram_tensor("cd", ((UNITS + 1) * P, QH), F32, kind="Internal").ap()

        cst = sb("cst", [P, C_ALL])
        zero = sb("zero", [P, D])
        ones = sb("ones", [P, P])
        bias = sb("bias", [P, D])
        ident = cst[:, C_ID:C_ID + P]
        tri = cst[:, C_TRI:C_TRI + P]
        cosT = cst[:, C_COS:C_COS + TB * DK].rearrange("p (t d) -> p t d", d=DK)
        sinT = cst[:, C_SIN:C_SIN + TB * DK].rearrange("p (t d) -> p t d", d=DK)
        tie = cst[:, C_TIE:C_TIE + E * E].rearrange("p (e f) -> p e f", f=E)
        big = sb("big", [P, (E + 1) * (KC * 2 * I + IC * D)])
        n_gu = (E + 1) * KC * 2 * I
        w_gu = big[:, 0:n_gu]
        w_dn = big[:, n_gu:n_gu + (E + 1) * IC * D]
        GU, DN = KC * 2 * I, IC * D
        probs = big[:, 0:8 * 2 * QH].rearrange("p (k h q) -> p k h q", k=8, h=2)
        acc = big[:, 8192:12288].rearrange("p (u a h q) -> p u a h q", u=2, a=2, h=2)
        ctx_raw = big[:, 12288:13312].rearrange("p (r q) -> p r q", r=2)
        ctx_nrm = big[:, 13312:14336].rearrange("p (r q) -> p r q", r=2)
        den = big[:, 14336:14848]
        rden = big[:, 14848:15360]
        y_pick = big[:, 15360:15360 + NT * 2 * D].rearrange("p (t s d) -> p t s d", t=NT, s=2)
        ct = big[:, 0:2 * 8 * P].rearrange("p (r c q) -> p r c q", r=2, c=8)
        wo = big[:, 2048:2048 + 8 * D].rearrange("p (c d) -> p c d", c=8)
        fx = big[:, 4096:4096 + 2 * D].rearrange("p (r d) -> p r d", r=2)
        fy = big[:, 4608:4608 + 2 * D].rearrange("p (r d) -> p r d", r=2)
        fa = big[:, 5120:5120 + 2 * D].rearrange("p (r d) -> p r d", r=2)
        fb = big[:, 5632:5632 + 2 * D].rearrange("p (r d) -> p r d", r=2)
        mid = sb("mid", [P, 4608])
        xs = mid[:, 0:NT * D].rearrange("p (t d) -> p t d", d=D)
        q_nat = mid[:, 0:4 * QT * P].rearrange("p (r t c) -> p r t c", r=4, t=QT)
        k_nat = mid[:, 2048:2048 + TB * 3 * ST].rearrange("p (t c) -> p t c", t=TB)
        v_nat = mid[:, 3584:3584 + 2 * TB * DV].rearrange("p (r t d) -> p r t d", r=2, t=TB)
        KT = sb("KT", [P, 2, 2, L], F32R)
        QT1 = sb("QT1", [P, 2, QH], F32R)
        QT2 = sb("QT2", [P, 2, QH], F32R)
        w_in = sb("w_in", [P, KC, QK_COLS + VG_COLS])
        wrk = sb("wrk", [P, 2 * (NHK * ST + NKV * DV + 3 * QK_COLS)])
        stack = wrk[:, 0:2560].rearrange("p (r h c) -> p r h c", r=2, h=NHK)
        v_out = wrk[:, 2560:3072].rearrange("p (r c) -> p r c", r=2)
        rope_a = wrk[:, 3072:3712].rearrange("p (r h c) -> p r h c", r=2, h=NHK)
        rope_b = wrk[:, 3712:4352].rearrange("p (r h c) -> p r h c", r=2, h=NHK)
        roped = wrk[:, 4352:4992].rearrange("p (r h c) -> p r h c", r=2, h=NHK)
        gate_t = wrk[:, 0:1024].rearrange("p (r c) -> p r c", r=2)
        gate_s = wrk[:, 1024:2048].rearrange("p (r c) -> p r c", r=2)
        hid = wrk[:, 2048:3072].rearrange("p (r c) -> p r c", r=2)
        hidT = wrk[:, 3072:4096].rearrange("p (r c) -> p r c", r=2)
        y_sb = wrk[:, 4096:4608].rearrange("p (r c) -> p r c", r=2)
        xt_in = sb("xt_in", [P, 2, D])
        xT = sb("xT", [P, 2, D])
        stats = sb("stats", [P, NT, 6])
        mv = sb("mv", [P, NT, 2])
        veps = sb("veps", [P, NT])
        std = sb("std", [P, NT])
        rstd = sb("rstd", [P, NT])
        mpart = sb("mpart", [P, 2, QT * 2 * 2])
        lg = sb("lg", [P, NT, E])
        r_gt = sb("r_gt", [P, NT * E * E])
        r_eq = sb("r_eq", [P, NT * E * E])
        rank = sb("rank", [P, NT, E])
        sel = sb("sel", [P, 3, NT, E])
        tmp = sb("tmp", [P, NT, E])
        best = sb("best", [P, 2, NT])
        wts = sb("wts", [P, 4, NT])
        cum = sb("cum", [P, 2, 8 + NT, E])
        cumt = sb("cumt", [P, 2, 4 + E])
        ntl = sb("ntl", [P, E])
        slotf = sb("slotf", [P, NT, E])
        posf = sb("posf", [P, 2, NT])
        pos = sb("pos", [P, 2, NT], I32)
        etf = sb("etf", [P, XTILES])
        etab = sb("etab", [P, 2 + XTILES], I32)

        ps_s = [ctx.enter_context(nc.psum_tensor(f"ps_s{i}", [P, 2 * 512], F32)) for i in range(2)]
        ps = [ctx.enter_context(nc.psum_tensor(f"ps{i}", [P, 512], F32)) for i in range(4, 8)]
        bank = [ps_s[0][:, 0:512], ps_s[0][:, 512:1024], ps_s[1][:, 0:512], ps_s[1][:, 512:1024]] + [p[:, :] for p in ps]
        ps_pass1, ps_ctx, ps_misc = bank[4:6], bank[6], bank[7]

        s_cst, s_x, s_win, s_wff, s_bias = sem("cst_in"), sem("x_in"), sem("w_in_in"), sem("w_ff_in"), sem("bias_in")
        s_mem = sem("constants_set")
        s_zero = sem("scratch_zeroed")
        s_bn, s_mv, s_veps, s_std, s_rstd = sem("bn_done"), sem("mv_done"), sem("veps_done"), sem("std_done"), sem("rstd_done")
        a_xn = sem("a_xn_ready")
        s_xd = sem("a_xn_in_dram")
        a_xl = [sem(f"a_xn_tile{i}") for i in range(2)]
        a_xtp, a_xt = sem("a_xT_in_psum"), sem("a_xT_ready")
        a_qk, a_vg = sem("a_qk_in_psum"), sem("a_vg_in_psum")
        a_vev = sem("a_v_evacuated")
        a_ra, a_rb = sem("a_rope_cos"), sem("a_rope_sin")
        a_ro, a_hi, a_lo = sem("a_roped"), sem("a_high_part"), sem("a_low_part")
        a_qst = [sem(f"a_qkv_stored{i}") for i in range(2)]
        r_ch, r_sel, r_cnt, r_d, r_e, r_pos = sem("r_chain"), sem("r_selected"), sem("r_counted"), sem("r_diff"), sem("r_exp"), sem("r_pos_ready")
        s_disp = sem("rows_dispatched")
        f_xl = [sem(f"f_x_loaded{i}") for i in range(2)]
        f_xtp, f_xt = sem("f_xT_in_psum"), sem("f_xT_ready")
        f_g, f_u, f_th, f_s, f_h = sem("f_gate_in_psum"), sem("f_up_in_psum"), sem("f_tanh"), sem("f_gate_silu"), sem("f_hidden")
        f_htp, f_ht, f_y, f_ye = sem("f_hT_in_psum"), sem("f_hT_ready"), sem("f_y_in_psum"), sem("f_y_evacuated")
        f_ys = [sem(f"f_y_stored{i}") for i in range(2)]
        t_q = [sem(f"t_q_loaded{i}") for i in range(4)]
        t_k, t_v = sem("t_k_loaded"), [sem(f"t_v_loaded{i}") for i in range(2)]
        t_kpad = sem("t_k_padding")
        t_misc, t_miscev = sem("t_misc_in_psum"), sem("t_misc_evacuated")
        t_p1, t_red, t_negm = sem("t_pass1_in_psum"), sem("t_pass1_reduced"), sem("t_negmax_ready")
        t_s, t_e, t_pv = sem("t_scores_in_psum"), sem("t_exp_done"), sem("t_pv_done")
        t_add, t_cev = sem("t_probs_added"), sem("t_ctx_evacuated")
        t_rd, t_nrm = sem("t_den_inverted"), sem("t_ctx_normalised")
        t_cst = [sem(f"t_ctx_stored{i}") for i in range(2)]
        t_set = sem("t_standin_set")
        o_w = sem("o_w_in")
        o_in = [sem(f"o_tile_in{i}") for i in range(2)]
        o_y = [sem(f"o_rows_picked{i}") for i in range(4)]
        o_mm, o_f, o_done = sem("o_in_psum"), sem("o_chain"), sem("o_ready")
        o_st = [sem(f"o_stored{i}") for i in range(2)]

        PRO = [(-3, "T1"), (-3, "K0"), (-3, "K1"), (-3, "K2"), (-3, "K3"), (-2, "T1"), (-1, "T1"), (-1, "T2")]
        SLOT = {"T1": 0, "K0": 1, "K2": 1, "T2": 3, "DEN": 4, "K1": 6, "K3": 6}
        BODY = []
        for lu in range(8):
            k = {0: ["K0", "K1"], 1: ["K2", "K3"]}.get(lu % 4, [])
            BODY += [(lu, n) for n in sorted(["T1", "T2", "DEN"] + k, key=lambda n: SLOT[n])]

        def misc_index(it, lu, name):
            if it is None:
                return PRO.index((lu, name)) if lu < 0 else len(PRO) + 4 * len(BODY)
            return it * len(BODY) + (len(PRO) + BODY.index((lu, name)))

        def before_unit(it, lu):
            if it is None:
                return {-2: 5, -1: 6}[lu]
            if lu == 0:
                return it * len(BODY) + len(PRO)
            return misc_index(it, lu - 1, "K3" if lu % 4 == 2 else "T2") + 1

        def misc_of(lu, kt):
            return [n for l, n in BODY if l == lu and SLOT[n] == kt]

        def at(it, lu, per, plus=0):
            return per * lu + plus if it is None else it * (8 * per) + (per * lu + plus)

        block = ctx.enter_context(nc.Block())

        @block.sync
        def _(sp):
            sp.dma_start(cst[:, :], consts).then_inc(s_cst, 16)
            xv = x.rearrange("b (t p) d -> p (b t) d", p=P)
            for j in range(4):
                sp.dma_start(xs[:, 4 * j:4 * j + 4, :], xv[:, 4 * j:4 * j + 4, :]).then_inc(s_x, 16)
            sp.dma_start(w_in[:, :, 0:QK_COLS + NKV * DV], w_attn.rearrange("(k p) n -> p k n", p=P)).then_inc(s_win, 16)
            sp.dma_start(w_in[:, :, QK_COLS + NKV * DV:], gate_w.rearrange("(k p) n -> p k n", p=P)).then_inc(s_win, 16)
            sp.dma_start(bias[:, :], b_out.partition_broadcast(P)).then_inc(s_bias, 16)
            sp.wait_ge(a_xn, NT)
            sp.dma_start(xd[0:TOK, :].rearrange("(t p) d -> p t d", p=P), xs[:, :, :]).then_inc(s_xd, 16)
            for b in range(B):
                qb = qd[b * PAIRS * L:(b + 1) * PAIRS * L, :].rearrange("(c t) e -> t c e", c=PAIRS)
                kb = kd[b * NKV * L:(b + 1) * NKV * L, :].rearrange("(c t) e -> t c e", c=NKV)
                vb = vd[b * NKV * L:(b + 1) * NKV * L, :].rearrange("(c t) e -> t c e", c=NKV)
                with sp.Fori(0, TB // 2) as i:
                    for h in range(2):
                        t = i * 2 + (b * TB + h)
                        sp.wait_ge(a_xtp, t + 1)
                        sp.dma_start(xt_in[:, h:h + 1, :], xs[:, ds(t, 1), :]).then_inc(a_xl[h], 16)
                        row = i * (2 * P) + h * P
                        sp.wait_ge(a_vev, t + 1)
                        sp.dma_start(vb[ds(row, P), :, :], v_out[:, h, :].rearrange("p (c d) -> p c d", c=NKV)).then_inc(a_qst[h], 16)
                        sp.wait_ge(a_lo, 2 * t + 2)
                        sp.dma_start(qb[ds(row, P), :, :], stack[:, h, 0:NH, :].rearrange("p (c e) k -> p c (e k)", c=PAIRS)).then_inc(a_qst[h], 16)
                        sp.dma_start(kb[ds(row, P), :, :], stack[:, h, NH:NHK, :]).then_inc(a_qst[h], 16)

            def load_x(n, h):
                sp.wait_ge(f_xtp, n - 1)
                sp.dma_start(xt_in[:, h, :], xd[ds(n * P, P), :]).then_inc(f_xl[h], 16)

            def store_y(n, h):
                sp.wait_ge(f_ye, n + 1)
                sp.dma_start(yd[ds(n * P, P), :], y_sb[:, h, :]).then_inc(f_ys[h], 16)

            sp.wait_ge(s_xd, 16)
            sp.wait_ge(a_xtp, NT + 2)
            for n in range(2):
                sp.dma_start(xt_in[:, n, :], xd[n * P:(n + 1) * P, :]).then_inc(f_xl[n], 16)
            load_x(2, 0)
            with sp.Fori(0, (NT - 4) // 2) as i:
                for h in range(2):
                    n = i * 2 + (1 + h)
                    load_x(n + 2, (1 + h) % 2)
                    store_y(n - 1, h)
            load_x(NT - 1, 1)
            store_y(NT - 4, 0)
            sp.wait_ge(s_disp, 16 * 2 * NT)
            with sp.Fori(0, (NF - NT) // 2) as i:
                for h in range(2):
                    n = i * 2 + (NT - 2 + h)
                    load_x(n + 2, h)
                    store_y(n - 1, (1 + h) % 2)
            for n in (NF - 3, NF - 2, NF - 1):
                store_y(n, n % 2)

            def load_q(v, r):
                sp.dma_start(q_nat[:, r, :, :], qd[ds(v * QH, QH), :].rearrange("(t p) c -> p t c", p=P)).then_inc(t_q[r], 16)

            def load_k(g):
                sp.dma_start(k_nat[:, :, ST:2 * ST], kd[ds(g * L, L), :].rearrange("(t p) c -> p t c", p=P)).then_inc(t_k, 16)

            def load_v(g, r):
                sp.dma_start(v_nat[:, r, :, :], vd[ds(g * L, L), :].rearrange("(t p) c -> p t c", p=P)).then_inc(t_v[r], 16)

            for h in range(2):
                sp.wait_ge(a_qst[h], 16 + 48 * (NT // 2))
            sp.wait_ge(s_zero, 64)
            load_q(0, 0)
            load_k(0)
            for v in range(1, 4):
                load_q(v, v)
            load_v(0, 0)
            sp.wait_ge(t_misc, 5)
            load_k(1)
            with sp.Fori(0, UNITS // 8) as it:
                for lu in range(8):
                    sp.wait_ge(t_misc, before_unit(it, lu))
                    load_q(at(it, lu, 1, 4), lu % 4)
                    if lu % 4 == 0:
                        sp.wait_ge(t_pv, at(it, lu, 8, 8))
                        load_v(it * 2 + (lu // 4 + 1), (lu // 4 + 1) % 2)
                    if lu % 4 == 2:
                        sp.wait_ge(t_misc, misc_index(it, lu - 1, "K3") + 1)
                        load_k(it * 2 + (lu // 4 + 2))
                    sp.wait_ge(t_nrm, at(it, lu, 1, 3))
                    sp.dma_start(cd[ds(at(it, lu, 1) * P, P), :], ctx_nrm[:, (lu + 1) % 2, :]).then_inc(t_cst[(lu + 1) % 2], 16)
            sp.wait_ge(t_nrm, UNITS + 3)
            sp.dma_start(cd[UNITS * P:(UNITS + 1) * P, :], ctx_nrm[:, 1, :]).then_inc(t_cst[1], 16)

            sp.wait_ge(t_pv, 8 * UNITS + 8)
            sp.wait_ge(t_add, 6 * UNITS + 6)
            sp.dma_start(wo, w_out.rearrange("(c p) d -> p c d", p=P)).then_inc(o_w, 16)
            sp.wait_ge(t_cst[0], 16 + 16 * (UNITS // 2))
            sp.wait_ge(t_cst[1], 16 + 16 * (UNITS // 2 + 1))
            for h in range(2):
                sp.wait_ge(f_ys[h], 16 + 16 * (NF // 2))
            xo = x.rearrange("b (t p) d -> (b t) p d", p=P)
            for t in range(NT):
                b, tb = divmod(t, TB)
                if t >= 2:
                    sp.wait_ge(o_mm, t - 1)
                    sp.wait_ge(o_done, t - 1)
                half, q0 = divmod(tb, QT)
                src = cd[P * (1 + b * 16):P * (1 + (b + 1) * 16), :].rearrange("(c s p) q -> s p c q", s=2, p=P)
                sp.dma_start(ct[:, t % 2, :, :], src[half, :, :, q0 * P:(q0 + 1) * P]).then_inc(o_in[t % 2], 16)
                sp.dma_start(fx[:, t % 2, :], xo[t]).then_inc(o_in[t % 2], 16)
                sp.dma_start(fy[:, t % 2, :], yd[t * P:(t + 1) * P, :]).then_inc(o_in[t % 2], 16)

        @block.gpsimd
        def _(pool):
            nc.gpsimd.memset(zero[:, :], 0.0).then_inc(s_mem, 1)
            nc.gpsimd.memset(ones[:, :], 1.0).then_inc(s_mem, 1)
            nc.gpsimd.memset(stack[:, :, :, MCOL:], 0.0).then_inc(s_mem, 1)
            pool.wait_ge(s_mem, 3)
            nc.gpsimd.memset(stack[:, :, NH:, MCOL:MCOL + 1], 1.0).then_inc(s_mem, 1)
            nc.gpsimd.memset(cum[:, :, :, :], 0.0).then_inc(s_mem, 1)
            nc.gpsimd.memset(cumt[:, :, :], 0.0).then_inc(s_mem, 1)
            nc.gpsimd.memset(etab[:, 0:2], E).then_inc(s_mem, 1)
            pool.wait_ge(s_mem, 7)
            for b in range(B):
                with pool.Fori(0, TB // 2) as i:
                    for h in range(2):
                        t = i * 2 + (b * TB + h)
                        pool.wait_ge(a_hi, 2 * t + 2)
                        nc.gpsimd.tensor_tensor(stack[:, h, 0:NH, 2 * DK:3 * DK].bitcast(F32R), roped[:, h, 0:NH, :],
                                                stack[:, h, 0:NH, 0:DK], ALU.subtract).then_inc(a_lo, 1)
                        nc.gpsimd.tensor_tensor(stack[:, h, NH:, DK:2 * DK].bitcast(F32R), roped[:, h, NH:, :],
                                                stack[:, h, NH:, 0:DK], ALU.subtract).then_inc(a_lo, 1)
            pool.wait_ge(s_zero, 64)
            pool.wait_ge(s_xd, 16)
            pool.wait_ge(r_pos, 2)
            for h in range(2):
                pool.wait_ge(a_xl[h], 16 * (NT // 2))
            for t in range(NT):
                for s in range(2):
                    pool.indirect_dma_start(xd, bass.IndirectOffsetOnAxis(ap=pos[:, s, t:t + 1], axis=0),
                                            xs[:, t, :], None).then_inc(s_disp, 16)
            pool.wait_ge(s_disp, 16 * 2 * NT)
            nc.gpsimd.memset(k_nat[:, :, 0:ST], 0.0).then_inc(t_kpad, 1)
            nc.gpsimd.memset(k_nat[:, :, 2 * ST:], 0.0).then_inc(t_kpad, 1)
            nc.gpsimd.memset(v_nat[:, 1, :, :], 0.0).then_inc(t_set, 1)
            pool.wait_ge(f_y, NF)
            nc.gpsimd.memset(probs[:, 0, :, :], 1.0).then_inc(t_set, 1)
            nc.gpsimd.memset(probs[:, 7, :, :], 1.0).then_inc(t_set, 1)
            nc.gpsimd.memset(acc[:, 1, :, :, :], 1.0).then_inc(t_set, 1)
            pool.sem_inc(t_add, 6)
            with pool.Fori(0, UNITS // 8) as it:
                for lu in range(8):
                    u2 = lu % 2
                    for a, (first, kt) in enumerate([(0, 1), (2, 3), (None, 4), (None, 5), (None, 6), (None, 7)]):
                        pool.wait_ge(t_e, at(it, lu, 8, kt + 3))
                        o = acc[:, u2, a % 2, :, :]
                        if first is None:
                            pool.wait_ge(t_add, at(it, lu, 6, 6 + a - 1))
                            nc.gpsimd.tensor_tensor(o, o, probs[:, kt, :, :], ALU.add).then_inc(t_add, 1)
                        else:
                            if a == 0:
                                if lu:
                                    pool.wait_ge(t_misc, misc_index(it, lu - 1, "DEN") + 1)
                                else:
                                    pool.wait_ge(t_misc, it * len(BODY) + len(PRO))
                            nc.gpsimd.tensor_tensor(o, probs[:, first, :, :], probs[:, kt, :, :], ALU.add).then_inc(t_add, 1)
            for h in range(2):
                pool.wait_ge(f_ys[h], 16 + 16 * (NF // 2))
            for t in range(NT):
                for s in range(2):
                    pool.indirect_dma_start(y_pick[:, t, s, :], None, yd,
                                            bass.IndirectOffsetOnAxis(ap=pos[:, s, t:t + 1], axis=0)).then_inc(o_y[t % 4], 16)
                if t >= 3:
                    pool.wait_ge(o_y[(t - 3) % 4], 32 * ((t - 3) // 4 + 1))

        @block.scalar
        def _(act):
            act.wait_ge(s_mem, 1)
            act.dma_start(xd[TOK:ROWS, :].rearrange("(k p) d -> p k d", p=P),
                          zero[:, :].unsqueeze(1).to_broadcast([P, XTILES, D])).then_inc(s_zero, 16)
            act.dma_start(qd[GROUPS * 2 * L:, :].rearrange("(k p) d -> p k d", p=P),
                          zero[:, 0:P].unsqueeze(1).to_broadcast([P, 2 * L // P, P])).then_inc(s_zero, 16)
            act.dma_start(kd[GROUPS * L:, :].rearrange("(k p) d -> p k d", p=P),
                          zero[:, 0:ST].unsqueeze(1).to_broadcast([P, 2 * L // P, ST])).then_inc(s_zero, 16)
            act.dma_start(vd[GROUPS * L:, :].rearrange("(k p) d -> p k d", p=P),
                          zero[:, 0:DV].unsqueeze(1).to_broadcast([P, L // P, DV])).then_inc(s_zero, 16)
            order = [E] + list(range(E))
            for e in order:
                gu, dn = (base_gu, base_dn) if e == E else (exp_gu[e], exp_dn[e])
                act.dma_start(w_gu[:, e * GU:(e + 1) * GU].rearrange("p (k n) -> p k n", k=KC),
                              gu.rearrange("(k p) n -> p k n", p=P)).then_inc(s_wff, 16)
                act.dma_start(w_dn[:, e * DN:(e + 1) * DN].rearrange("p (k n) -> p k n", k=IC),
                              dn.rearrange("(k p) n -> p k n", p=P)).then_inc(s_wff, 16)
            for h in range(2):
                act.sem_inc(a_qst[h], 16)
                act.sem_inc(f_ys[h], 16)
                act.sem_inc(t_cst[h], 16)
                act.sem_inc(o_st[h], 16)
            act.sem_inc(t_e, 2)
            act.sem_inc(t_pv, 6)
            act.sem_inc(t_nrm, 2)
            act.wait_ge(s_veps, 1)
            nc.scalar.activation(std[:, :], veps[:, :], ACT.Sqrt).then_inc(s_std, 1)
            act.sem_inc(a_vg, 2)
            act.sem_inc(a_xtp, 2)
            act.sem_inc(a_ro, 2)
            for b in range(B):
                with act.Fori(0, TB // 2) as i:
                    for h in range(2):
                        t = i * 2 + (b * TB + h)
                        act.wait_ge(a_xtp, t + 3)
                        act.wait_ge(a_vg, t + 1)
                        nc.scalar.activation(xT[:, h, :], bank[0][:, 0:D], ACT.Copy).then_inc(a_xt, 1)
                        act.wait_ge(a_vg, t + 3)
                        act.wait_ge(a_qst[h], i * 48 + (16 + 48 * 4 * b))
                        nc.scalar.activation(v_out[:, h, :], bank[3 + h][:, 0:NKV * DV], ACT.Copy)
                        nc.scalar.activation(lg[:, ds(t, 1), :],
                                             bank[3 + h][:, NKV * DV:VG_COLS].unsqueeze(1), ACT.Copy).then_inc(a_vev, 1)
                        act.wait_ge(a_ro, t + 3)
                        nc.scalar.activation(stack[:, h, 0:NH, 0:2 * DK].rearrange("p h (c k) -> p h c k", c=2).bitcast(F32R),
                                             roped[:, h, 0:NH, :].unsqueeze(2).to_broadcast([P, NH, 2, DK]), ACT.Copy).then_inc(a_hi, 1)
                        nc.scalar.activation(stack[:, h, NH:, 0:4 * DK].rearrange("p h (c k) -> p h c k", c=2)[:, :, :, 0:DK].bitcast(F32R),
                                             roped[:, h, NH:, :].unsqueeze(2).to_broadcast([P, NKV, 2, DK]), ACT.Copy).then_inc(a_hi, 1)
            act.wait_ge(r_d, 1)
            nc.scalar.activation(wts[:, 1, :], wts[:, 0, :], ACT.Exp).then_inc(r_e, 1)

            for h in range(2):
                act.wait_ge(a_qst[h], 16 + 48 * (NT // 2))

            def ev_xT(n, h):
                act.wait_ge(f_xtp, n + 1)
                nc.scalar.activation(xT[:, h, :], bank[0][:, 0:D], ACT.Copy).then_inc(f_xt, 1)

            def tanh(n, h):
                act.wait_ge(f_g, n + 1)
                nc.scalar.activation(gate_t[:, h, :], bank[1 + 2 * h], ACT.Tanh, scale=0.5).then_inc(f_th, 1)

            def ev_hT(n, h):
                act.wait_ge(f_htp, n + 1)
                nc.scalar.activation(hidT[:, h, :], bank[5], ACT.Copy).then_inc(f_ht, 1)

            ev_xT(0, 0)
            tanh(0, 0)
            ev_xT(1, 1)

            def act_step(n, h):
                tanh(n, h)
                ev_hT(n - 1, 1 - h)
                act.wait_ge(f_u, n)
                ev_xT(n + 1, 1 - h)

            with act.Fori(0, (NF - 2) // 2) as i:
                for h in range(2):
                    act_step(i * 2 + (1 + h), 1 - h)
            tanh(NF - 1, 1)
            ev_hT(NF - 2, 0)
            ev_hT(NF - 1, 1)

            def ev_misc(it, lu, name):
                act.wait_ge(t_misc, misc_index(it, lu, name) + 1)
                if name == "T1":
                    dst = QT1[:, (lu + 3) % 2, :]
                elif name == "T2":
                    dst = QT2[:, (lu + 1) % 2, :]
                elif name == "DEN":
                    act.wait_ge(t_nrm, at(it, lu, 1, 2))
                    dst = den
                else:
                    g2 = 0 if lu < 0 else (lu // 4 + 1) % 2
                    k = int(name[1])
                    dst = KT[:, g2, k // 2, (k % 2) * 512:(k % 2 + 1) * 512]
                nc.scalar.activation(dst, ps_misc, ACT.Copy).then_inc(t_miscev, 1)

            ADDS = [1, 1, 2, 2, 3, 4, 5, 6]
            for lu, name in PRO:
                ev_misc(None, lu, name)
            with act.Fori(0, UNITS // 8) as it:
                for lu in range(8):
                    for kt in range(8):
                        act.wait_ge(t_s, at(it, lu, 8, kt + 1))
                        act.wait_ge(t_pv, at(it, lu, 8, kt + 1))
                        act.wait_ge(t_add, at(it, lu, 6, ADDS[kt]))
                        nc.scalar.activation(probs[:, kt, :, :], ps_s[kt % 2][:, :].rearrange("p (h q) -> p h q", h=2),
                                             ACT.Exp, scale=SCALE).then_inc(t_e, 1)
                        if kt == 0:
                            act.wait_ge(t_pv, at(it, lu, 8, 8))
                            act.wait_ge(t_nrm, at(it, lu, 1, 1))
                            nc.scalar.activation(ctx_raw[:, (lu + 1) % 2, :], ps_ctx, ACT.Copy).then_inc(t_cev, 1)
                        for name in misc_of(lu, kt):
                            ev_misc(it, lu, name)
            act.wait_ge(t_pv, 8 * UNITS + 8)
            act.wait_ge(t_nrm, UNITS + 1)
            nc.scalar.activation(ctx_raw[:, 1, :], ps_ctx, ACT.Copy).then_inc(t_cev, 1)
            act.wait_ge(t_misc, len(PRO) + 4 * len(BODY) + 1)
            act.wait_ge(t_nrm, UNITS + 2)
            nc.scalar.activation(den, ps_misc, ACT.Copy).then_inc(t_miscev, 1)

            ov = out.rearrange("b (t p) d -> (b t) p d", p=P)
            for t in range(NT):
                act.wait_ge(o_done, t + 1)
                act.dma_start(ov[t], fb[:, t % 2, :]).then_inc(o_st[t % 2], 16)
            for h in range(2):
                act.wait_ge(o_st[h], 16 + 16 * (NT // 2))

        @block.vector
        def _(dve):
            dve.wait_ge(s_x, 64)
            for t in range(NT):
                nc.vector.bn_stats(stats[:, t, :], xs[:, t, :]).then_inc(s_bn, 1)
            for t in range(NT):
                dve.wait_ge(s_bn, t + 1)
                nc.vector.bn_aggr(mv[:, t, :], stats[:, t, :]).then_inc(s_mv, 1)
            dve.wait_ge(s_mv, NT)
            nc.vector.tensor_scalar(veps[:, :], mv[:, :, 1], EPS, None, ALU.add).then_inc(s_veps, 1)
            dve.wait_ge(s_std, 1)
            nc.vector.reciprocal(rstd[:, :], std[:, :]).then_inc(s_rstd, 1)
            dve.wait_ge(s_rstd, 1)
            dve.wait_ge(s_cst, 16)
            for t in range(NT):
                nc.vector.tensor_scalar(xs[:, t, :], xs[:, t, :], mv[:, t, 0:1], rstd[:, t:t + 1],
                                        ALU.subtract, ALU.mult).then_inc(a_xn, 1)
            for b in range(B):
                with dve.Fori(0, TB // 2) as i:
                    for h in range(2):
                        t = i * 2 + (b * TB + h)
                        dve.wait_ge(a_qk, t + 1)
                        qk = bank[1 + h][:, 0:QK_COLS].rearrange("p (h c) -> p h c", c=DK)
                        tb = i * 2 + h
                        H2 = DK // 2
                        cs = cosT[:, ds(tb, 1), :].to_broadcast([P, NHK, DK])
                        sn = sinT[:, ds(tb, 1), :].to_broadcast([P, NHK, DK])
                        nc.vector.tensor_tensor(rope_a[:, h, :, :], qk, cs, ALU.mult).then_inc(a_ra, 1)
                        nc.vector.tensor_tensor(rope_b[:, h, :, 0:H2], qk[:, :, H2:], sn[:, :, 0:H2], ALU.mult).then_inc(a_rb, 1)
                        nc.vector.tensor_tensor(rope_b[:, h, :, H2:], qk[:, :, 0:H2], sn[:, :, H2:], ALU.mult).then_inc(a_rb, 1)
                        dve.wait_ge(a_ra, t + 1)
                        dve.wait_ge(a_rb, 2 * t + 2)
                        dve.wait_ge(a_qst[h], i * 48 + (16 + 48 * 4 * b))
                        nc.vector.tensor_tensor(roped[:, h, :, :], rope_a[:, h, :, :], rope_b[:, h, :, :], ALU.add).then_inc(a_ro, 1)

            steps = [0]

            def link(ins):
                steps[0] += 1
                ins.then_inc(r_ch, 1)
                dve.wait_ge(r_ch, steps[0])

            dve.wait_ge(a_vev, NT)
            dve.wait_ge(s_mem, 7)
            V = nc.vector
            full = [P, NT, E, E]
            gt4 = r_gt[:, :].rearrange("p (t e f) -> p t e f", e=E, f=E)
            eq4 = r_eq[:, :].rearrange("p (t e f) -> p t e f", e=E, f=E)
            l_f = lg[:, :, :].unsqueeze(2).to_broadcast(full)
            l_e = lg[:, :, :].unsqueeze(3).to_broadcast(full)
            link(V.tensor_tensor(gt4, l_f, l_e, ALU.is_gt))
            link(V.tensor_tensor(eq4, l_f, l_e, ALU.is_equal))
            link(V.tensor_tensor(eq4, eq4, tie.unsqueeze(1).to_broadcast(full), ALU.mult))
            link(V.tensor_tensor(r_gt[:, :], r_gt[:, :], r_eq[:, :], ALU.add))
            link(V.tensor_reduce(rank[:, :, :], gt4, AX.X, ALU.add))
            for s in range(2):
                link(V.tensor_scalar(sel[:, s, :, :], rank[:, :, :], float(s), None, ALU.is_equal))
                link(V.tensor_tensor(tmp[:, :, :], sel[:, s, :, :], lg[:, :, :], ALU.mult))
                link(V.tensor_reduce(best[:, s, :], tmp[:, :, :], AX.X, ALU.add))
            V.tensor_tensor(sel[:, 2, :, :], sel[:, 0, :, :], sel[:, 1, :, :], ALU.add).then_inc(r_sel, 1)
            V.tensor_tensor(wts[:, 0, :], best[:, 1, :], best[:, 0, :], ALU.subtract).then_inc(r_d, 1)
            dve.wait_ge(r_e, 1)
            link(V.tensor_scalar(wts[:, 3, :], wts[:, 1, :], 1.0, None, ALU.add))
            link(V.reciprocal(wts[:, 2, :], wts[:, 3, :]))
            link(V.tensor_tensor(wts[:, 3, :], wts[:, 1, :], wts[:, 2, :], ALU.mult))
            dve.wait_ge(r_cnt, 1)
            pre = bank[5][:, 0:NT * E].rearrange("p (t e) -> p t e", e=E)
            tot = bank[5][:, NT * E:2 * NT * E].rearrange("p (t e) -> p t e", e=E)
            link(V.tensor_copy(tmp[:, :, :], tot))
            link(V.tensor_copy(cum[:, 0, 8:, :], tmp[:, :, :]))
            src = 0
            for sh in (1, 2, 4, 8):
                link(V.tensor_tensor(cum[:, 1 - src, 8:, :], cum[:, src, 8:, :], cum[:, src, 8 - sh:8 + NT - sh, :], ALU.add))
                src = 1 - src
            thr = cst[:, C_THR:C_THR + NT].unsqueeze(1).to_broadcast([P, E, NT])
            cmp = r_gt[:, 0:E * NT].rearrange("p (e k) -> p e k", e=E)
            cnt = cum[:, src, 8 + NT - 1, :].unsqueeze(2).to_broadcast([P, E, NT])
            link(V.tensor_tensor(cmp, cnt, thr, ALU.is_gt))
            link(V.tensor_reduce(ntl[:, :], cmp, AX.X, ALU.add))
            link(V.tensor_copy(cumt[:, 0, 4:], ntl[:, :]))
            s2 = 0
            for sh in (1, 2, 4):
                link(V.tensor_tensor(cumt[:, 1 - s2, 4:], cumt[:, s2, 4:], cumt[:, s2, 4 - sh:4 + E - sh], ALU.add))
                s2 = 1 - s2
            cm2 = r_eq[:, 0:XTILES * E].rearrange("p (k e) -> p k e", e=E)
            link(V.tensor_tensor(cm2, cumt[:, s2, 4:].unsqueeze(1).to_broadcast([P, XTILES, E]),
                                 cst[:, C_TIX:C_TIX + XTILES].unsqueeze(2).to_broadcast([P, XTILES, E]), ALU.is_le))
            link(V.tensor_reduce(etf[:, :], cm2, AX.X, ALU.add))
            link(V.tensor_scalar(etab[:, 2:], etf[:, :], float(E - 1), None, ALU.min))
            link(V.tensor_tensor(ntl[:, :], cumt[:, s2, 4:], ntl[:, :], ALU.subtract))
            link(V.tensor_scalar(ntl[:, :], ntl[:, :], float(P), float(TOK), ALU.mult, ALU.add))
            link(V.tensor_tensor(slotf[:, :, :], cum[:, src, 8:, :], tmp[:, :, :], ALU.subtract))
            link(V.tensor_tensor(slotf[:, :, :], slotf[:, :, :], pre, ALU.add))
            link(V.tensor_tensor(slotf[:, :, :], slotf[:, :, :], ntl[:, :].unsqueeze(1).to_broadcast([P, NT, E]), ALU.add))
            for s in range(2):
                link(V.tensor_tensor(tmp[:, :, :], sel[:, s, :, :], slotf[:, :, :], ALU.mult))
                link(V.tensor_reduce(posf[:, s, :], tmp[:, :, :], AX.X, ALU.add))
                V.tensor_copy(pos[:, s, :], posf[:, s, :]).then_inc(r_pos, 1)

            def gate(n, h):
                dve.wait_ge(f_th, n + 1)
                V.scalar_tensor_tensor(gate_s[:, h, :], gate_t[:, h, :], 1.0, bank[1 + 2 * h], ALU.add, ALU.mult).then_inc(f_s, 1)
                dve.wait_ge(f_s, n + 1)
                dve.wait_ge(f_u, n + 1)
                V.scalar_tensor_tensor(hid[:, h, :], gate_s[:, h, :], 0.5, bank[2 + 2 * h], ALU.mult, ALU.mult).then_inc(f_h, 1)

            def ev_y(n, h):
                dve.wait_ge(f_y, n + 1)
                V.tensor_copy(y_sb[:, h, :], bank[6][:, 0:D]).then_inc(f_ye, 1)

            gate(0, 0)
            with dve.Fori(0, (NF - 2) // 2) as i:
                for h in range(2):
                    n = i * 2 + (1 + h)
                    gate(n, 1 - h)
                    dve.wait_ge(f_ys[h], i * 16 + 16)
                    ev_y(n - 1, h)
            gate(NF - 1, 1)
            dve.wait_ge(f_ys[0], 16 * ((NF - 2) // 2 + 1))
            ev_y(NF - 2, 0)
            dve.wait_ge(f_ys[1], 16 * ((NF - 2) // 2 + 1))
            ev_y(NF - 1, 1)

            def reduce(it, lu, j):
                dve.wait_ge(t_p1, at(it, lu + 2, 16, j + 1))
                V.tensor_reduce(mpart[:, lu % 2, j:j + 1], ps_pass1[j % 2], AX.X, ALU.max).then_inc(t_red, 1)

            def negmax(it, lu):
                dve.wait_ge(t_red, at(it, lu + 2, 16, 16))
                V.tensor_reduce(q_nat[:, (lu + 2) % 4, :, :].rearrange("p t (e c) -> p t e c", e=2)[:, :, :, MCOL].bitcast(F32R),
                                mpart[:, lu % 2, :].rearrange("p (t e k) -> p t e k", e=2, k=2),
                                AX.X, ALU.max, negate=True).then_inc(t_negm, 1)

            def invert(it, lu, c):
                if c == 0:
                    dve.wait_ge(t_miscev, misc_index(it, lu, "DEN") + 1)
                V.reciprocal(rden[:, c * P:(c + 1) * P], den[:, c * P:(c + 1) * P]).then_inc(t_rd, 1)

            def normalise(it, lu):
                dve.wait_ge(t_rd, at(it, lu, 4, 4))
                dve.wait_ge(t_cev, at(it, lu, 1, 1))
                dve.wait_ge(t_cst[(lu + 1) % 2], 16 * (lu // 2) + 16 if it is None else it * 64 + (16 * (lu // 2) + 16))
                V.tensor_tensor(ctx_nrm[:, (lu + 1) % 2, :], ctx_raw[:, (lu + 1) % 2, :], rden, ALU.mult).then_inc(t_nrm, 1)

            for lu in (-2, -1):
                for j in range(16):
                    reduce(None, lu, j)
                negmax(None, lu)
            with dve.Fori(0, UNITS // 8) as it:
                for lu in range(8):
                    for kt in range(8):
                        reduce(it, lu, 2 * kt)
                        reduce(it, lu, 2 * kt + 1)
                        if kt >= 5:
                            invert(it, lu, kt - 5)
                    negmax(it, lu)
                    invert(it, lu, 3)
                    normalise(it, lu)
            for c in range(4):
                invert(None, UNITS, c)
            normalise(None, UNITS)

            f = [0]

            def olink(ins):
                f[0] += 1
                ins.then_inc(o_f, 1)
                dve.wait_ge(o_f, f[0])

            dve.wait_ge(s_bias, 16)
            for t in range(NT):
                h = t % 2
                dve.wait_ge(o_in[h], 48 * (t // 2 + 1))
                olink(V.tensor_tensor(fa[:, h, :], fx[:, h, :], fy[:, h, :], ALU.add))
                olink(V.tensor_tensor(fa[:, h, :], fa[:, h, :], bias[:, :], ALU.add))
                dve.wait_ge(o_y[t % 4], 32 * (t // 4 + 1))
                olink(V.scalar_tensor_tensor(fa[:, h, :], y_pick[:, t, 0, :], wts[:, 2, t:t + 1], fa[:, h, :], ALU.mult, ALU.add))
                olink(V.scalar_tensor_tensor(fa[:, h, :], y_pick[:, t, 1, :], wts[:, 3, t:t + 1], fa[:, h, :], ALU.mult, ALU.add))
                dve.wait_ge(o_mm, t + 1)
                dve.wait_ge(o_st[h], 16 * (t // 2 + 1))
                V.tensor_tensor(fb[:, h, :], fa[:, h, :], bank[h][:, 0:D], ALU.add).then_inc(o_done, 1)

        @block.tensor
        def _(pe):
            mm = nc.tensor.matmul
            tr = nc.tensor.transpose
            pe.wait_ge(s_cst, 16)
            pe.wait_ge(s_win, 32)
            for b in range(B):
                with pe.Fori(0, TB // 2) as i:
                    for h in range(2):
                        t = i * 2 + (b * TB + h)
                        pe.wait_ge(a_xl[h], i * 16 + (16 + 64 * b))
                        for k in range(KC):
                            last = tr(bank[0][:, k * P:(k + 1) * P], xt_in[:, h, k * P:(k + 1) * P], ident)
                        last.then_inc(a_xtp, 1)
                        pe.wait_ge(a_xt, t + 1)
                        pe.wait_ge(a_ro, t + 1)
                        for k in range(KC):
                            last = mm(bank[1 + h][:, 0:QK_COLS], xT[:, h, k * P:(k + 1) * P], w_in[:, k, 0:QK_COLS],
                                      start=k == 0, stop=k == KC - 1)
                        last.then_inc(a_qk, 1)
                        for k in range(KC):
                            last = mm(bank[3 + h][:, 0:VG_COLS], xT[:, h, k * P:(k + 1) * P], w_in[:, k, QK_COLS:],
                                      start=k == 0, stop=k == KC - 1)
                        last.then_inc(a_vg, 1)
            pe.wait_ge(r_sel, 1)
            pe.wait_ge(s_mem, 2)
            sflat = sel[:, 2, :, :].rearrange("p t e -> p (t e)")
            mm(bank[5][:, 0:NT * E], tri, sflat, start=True, stop=True)
            mm(bank[5][:, NT * E:2 * NT * E], ones[:, :], sflat, start=True, stop=True).then_inc(r_cnt, 1)

            pe.wait_ge(a_ro, NT + 2)
            pe.wait_ge(a_vev, NT)
            pe.wait_ge(s_wff, 16 * 2 * (E + 1))
            pe.wait_ge(r_pos, 2)

            def x_T(n, h, l):
                pe.wait_ge(f_xl[h], l)
                pe.wait_ge(f_xt, n)
                for k in range(KC):
                    last = tr(bank[0][:, k * P:(k + 1) * P], xt_in[:, h, k * P:(k + 1) * P], ident)
                last.then_inc(f_xtp, 1)

            def up(n, h, half, e):
                for k in range(KC):
                    last = mm(bank[1 + 2 * h + half], xT[:, h, k * P:(k + 1) * P],
                              w_gu[:, ds(e * GU + (k * 2 * I + half * I), I)], start=k == 0, stop=k == KC - 1)
                last.then_inc((f_g, f_u)[half], 1)

            def h_T(n, h):
                pe.wait_ge(f_h, n + 1)
                for k in range(IC):
                    last = tr(bank[5][:, k * P:(k + 1) * P], hid[:, h, k * P:(k + 1) * P], ident)
                last.then_inc(f_htp, 1)

            def down(n, h, e):
                pe.wait_ge(f_ht, n + 1)
                for k in range(IC):
                    last = mm(bank[6][:, 0:D], hidT[:, h, k * P:(k + 1) * P], w_dn[:, ds(e * DN + k * D, D)],
                              start=k == 0, stop=k == IC - 1)
                last.then_inc(f_y, 1)

            def step(n, h, xl, e, e_before):
                pe.wait_ge(f_xt, n + 1)
                up(n, h, 0, e)
                h_T(n - 1, 1 - h)
                up(n, h, 1, e)
                x_T(n + 1, 1 - h, xl)
                pe.wait_ge(f_ye, n - 1) if not isinstance(n, int) or n > 1 else None
                down(n - 1, 1 - h, e_before)

            pe.wait_ge(f_xl[0], 16)
            for k in range(KC):
                last = tr(bank[0][:, k * P:(k + 1) * P], xt_in[:, 0, k * P:(k + 1) * P], ident)
            last.then_inc(f_xtp, 1)
            pe.wait_ge(f_xt, 1)
            up(0, 0, 0, E)
            up(0, 0, 1, E)
            x_T(1, 1, 16)
            step(1, 1, 32, E, E)
            step(2, 0, 32, E, E)
            with pe.Fori(0, (NT - 4) // 2) as i:
                for h in range(2):
                    step(i * 2 + (3 + h), 1 - h, i * 16 + 48, E, E)
            with pe.Fori(0, (NF - NT) // 2) as i:
                for h in range(2):
                    e0 = pe.value_load(etab[0:1, ds(i * 2 + h, 1)], min_val=0, max_val=E)
                    e1 = pe.value_load(etab[0:1, ds(i * 2 + (h + 1), 1)], min_val=0, max_val=E)
                    step(i * 2 + (NT - 1 + h), 1 - h, i * 16 + 16 * (NT // 2 + 1), e1, e0)
            e0 = pe.value_load(etab[0:1, XTILES:XTILES + 1], min_val=0, max_val=E)
            e1 = pe.value_load(etab[0:1, XTILES + 1:XTILES + 2], min_val=0, max_val=E)
            n = NF - 1
            pe.wait_ge(f_xt, NF)
            up(n, 1, 0, e1)
            h_T(n - 1, 0)
            up(n, 1, 1, e1)
            pe.wait_ge(f_ye, n - 1)
            down(n - 1, 0, e0)
            pe.wait_ge(f_ht, NF - 1)
            h_T(n, 1)
            pe.wait_ge(f_ye, n)
            down(n, 1, e1)

            def misc(it, lu, name):
                pe.wait_ge(t_miscev, misc_index(it, lu, name)) if not (it is None and (lu, name) == PRO[0]) else None
                if name == "T1":
                    v = lu + 3
                    cnt = v // 4 * 16 + 16 if it is None else it * 32 + (v // 4 * 16 + 16)
                    pe.wait_ge(t_q[v % 4], cnt)
                    for j in range(QT):
                        last = tr(ps_misc[:, j * P:(j + 1) * P], q_nat[:, v % 4, j, :], ident)
                elif name == "T2":
                    v = lu + 1
                    pe.wait_ge(t_negm, at(it, v, 1, 1))
                    for j in range(QT):
                        last = tr(ps_misc[:, j * P:(j + 1) * P], q_nat[:, v % 4, j, :], ident)
                elif name == "DEN":
                    pe.wait_ge(t_add, at(it, lu, 6, 6))
                    par = (lu - 1) % 2
                    for a in range(2):
                        for e in range(2):
                            last = mm(ps_misc[e * DV:(e + 1) * DV, :], ones[:, 0:DV], acc[:, par, a, e, :],
                                      start=a == 0, stop=a == 1)
                else:
                    k = int(name[1])
                    g1 = 16 if it is None else it * 32 + (lu // 4 * 16 + 32)
                    pe.wait_ge(t_k, g1)
                    var = k // 2
                    c0 = ST * (1 - var)
                    for j in range(QT):
                        last = tr(ps_misc[:, j * P:(j + 1) * P], k_nat[:, (k % 2) * QT + j, c0:c0 + P], ident)
                last.then_inc(t_misc, 1)

            def fill(it, lu, j):
                qt, e, kc = j // 4, j // 2 % 2, j % 2
                if not (it is None and lu == -2 and j < 2):
                    pe.wait_ge(t_red, at(it, lu + 2, 16, j - 1))
                if j == 0:
                    pe.wait_ge(t_miscev, before_unit(it, lu))
                g2 = (lu + 2) // 4 % 2
                mm(ps_pass1[j % 2], QT1[:, lu % 2, qt * P:(qt + 1) * P], KT[:, g2, e, kc * 512:(kc + 1) * 512],
                   start=True, stop=True).then_inc(t_p1, 1)

            def scores(it, lu, kt):
                pe.wait_ge(t_e, at(it, lu, 8, kt + 1))
                if kt == 0:
                    pe.wait_ge(t_miscev, before_unit(it, lu))
                g2 = lu // 4 % 2
                for e in range(2):
                    last = mm(ps_s[kt % 2][:, e * 512:(e + 1) * 512], KT[:, g2, e, kt * P:(kt + 1) * P], QT2[:, lu % 2, :],
                              start=True, stop=True)
                last.then_inc(t_s, 1)

            def weighted(it, lu, kt, start, stop):
                g2 = lu // 4 % 2
                for e in range(2):
                    last = mm(ps_ctx[e * DV:(e + 1) * DV, :], v_nat[:, g2, kt, :], probs[:, kt, e, :], start=start, stop=stop)
                last.then_inc(t_pv, 1)

            pe.wait_ge(t_kpad, 2)
            pe.wait_ge(f_ye, NF)
            for lu, name in PRO[:5]:
                misc(None, lu, name)
            for lu in (-2, -1):
                for name in [n for l, n in PRO if l == lu]:
                    misc(None, lu, name)
                for j in range(16):
                    fill(None, lu, j)
            pe.wait_ge(t_set, 4)
            weighted(None, -1, 0, True, False)
            with pe.Fori(0, UNITS // 8) as it:
                for lu in range(8):
                    for kt in range(8):
                        scores(it, lu, kt)
                        if kt == 0:
                            pe.wait_ge(t_e, at(it, lu, 8, 2))
                            weighted(it, lu - 1, 7, False, True)
                        fill(it, lu, 2 * kt)
                        fill(it, lu, 2 * kt + 1)
                        for name in misc_of(lu, kt):
                            misc(it, lu, name)
                        if kt:
                            pe.wait_ge(t_e, at(it, lu, 8, kt + 2))
                            if kt == 1:
                                pe.wait_ge(t_cev, at(it, lu, 1, 1))
                                pe.wait_ge(t_v[lu // 4 % 2], it * 16 + 16)
                            weighted(it, lu, kt - 1, kt == 1, False)
            pe.wait_ge(t_e, 8 * UNITS + 2)
            weighted(None, UNITS - 1, 7, False, True)
            pe.wait_ge(t_add, 6 * UNITS + 6)
            pe.wait_ge(t_miscev, len(PRO) + 4 * len(BODY))
            for a in range(2):
                for e in range(2):
                    last = mm(ps_misc[e * DV:(e + 1) * DV, :], ones[:, 0:DV], acc[:, 1, a, e, :], start=a == 0, stop=a == 1)
            last.then_inc(t_misc, 1)

            pe.wait_ge(o_w, 16)
            for t in range(NT):
                h = t % 2
                pe.wait_ge(o_in[h], 48 * (t // 2 + 1))
                if t >= 2:
                    pe.wait_ge(o_done, t - 1)
                for c in range(PAIRS):
                    last = mm(bank[h][:, 0:D], ct[:, h, c, :], wo[:, c, :], start=c == 0, stop=c == PAIRS - 1)
                last.then_inc(o_mm, 1)
    return nc


def make_consts():
    import numpy as np
    c = np.zeros((P, C_ALL), np.float32)
    c[:, C_ID:C_ID + P] = np.eye(P)
    c[:, C_TRI:C_TRI + P] = np.triu(np.ones((P, P)), 1)
    inv = (1.0 / np.float32(10000.0) ** (np.arange(0, DK, 2, dtype=np.float32) / np.float32(DK))).astype(np.float32)
    ang = np.arange(L, dtype=np.float32)[:, None] * inv[None, :]
    sin, cos = np.sin(ang).astype(np.float32), np.cos(ang).astype(np.float32)

    def tiles(a):
        return a.reshape(TB, P, DK).transpose(1, 0, 2).reshape(P, TB * DK)

    c[:, C_COS:C_COS + TB * DK] = tiles(np.concatenate([cos, cos], 1))
    c[:, C_SIN:C_SIN + TB * DK] = tiles(np.concatenate([-sin, sin], 1))
    c[:, C_TIE:C_TIE + E * E] = (np.arange(E)[None, :] < np.arange(E)[:, None]).astype(np.float32).reshape(-1)
    c[:, C_THR:C_THR + NT] = P * np.arange(NT)
    c[:, C_TIX:C_TIX + XTILES] = np.arange(XTILES)
    return c


_INS = ["L0_attn_x", "L0_attn_W_attn", "L0_attn_W_out", "L0_attn_b_out", "L0_ffn_gate_w", "L0_ffn_base_gate_up",
        "L0_ffn_base_down", "L0_ffn_expert_gate_up", "L0_ffn_expert_down"]


def kernel(**inputs):
    import numpy as np
    import concourse.bacc as bacc
    from concourse.bass_utils import run_bass_kernel_spmd

    nc = bacc.Bacc("TRN2", target_bir_lowering=False, num_devices=1)
    arrays, args = {}, []
    for name in _INS:
        a = np.ascontiguousarray(inputs[name])
        arrays[name] = a
        args.append(nc.dram_tensor(name, a.shape, mybir.dt.from_np(a.dtype), kind="ExternalInput").ap())
    arrays["consts"] = make_consts()
    args.append(nc.dram_tensor("consts", arrays["consts"].shape, mybir.dt.float32, kind="ExternalInput").ap())
    args.append(nc.dram_tensor("out", (B, L, D), mybir.dt.float32, kind="ExternalOutput").ap())
    build(nc, *args)
    r = run_bass_kernel_spmd(nc, [arrays], core_ids=[0])
    return r.results[0]["out"]
```

```python
from contextlib import ExitStack

import concourse.bass as bass
import concourse.mybir as mybir

P = 128
B, L, D = 2, 1024, 256
NH, NKV, DK, DV = 16, 4, 16, 64
E, I = 8, 512
TOK = B * L
NT = TOK // P
TB = L // P
KC = D // P
IC = I // P
NHK = NH + NKV
QK_COLS = NHK * DK
VG_COLS = NKV * DV + E
XTILES = 2 * NT + E
NF = NT + XTILES
ROWS = NF * P
ST = 64
MCOL = 48
PAIRS = NH // 2
GROUPS = B * NKV
QH = 512
QT = QH // P
UNITS = GROUPS * 2 * (L // QH)
EPS = 1e-5
SCALE = DK ** -0.5

C_ID, C_TRI, C_COS, C_SIN = 0, 128, 256, 384
C_TIE = 512
C_THR = C_TIE + E * E
C_TIX = C_THR + NT
C_ALL = C_TIX + XTILES


def build(nc, x, w_attn, w_out, b_out, gate_w, base_gu, base_dn, exp_gu, exp_dn, consts, out):
    F32, F32R, I32 = mybir.dt.float32, mybir.dt.float32r, mybir.dt.int32
    ALU, ACT, AX = mybir.AluOpType, mybir.ActivationFunctionType, mybir.AxisListType
    ds = bass.ds
    ctx = ExitStack()
    with ctx:
        def sb(name, shape, dt=F32):
            return ctx.enter_context(nc.sbuf_tensor(name, shape, dt))

        def sem(name):
            return ctx.enter_context(nc.semaphore(name))

        xd = nc.dram_tensor("xd", (ROWS, D), F32, kind="Internal").ap()
        yd = nc.dram_tensor("yd", (ROWS, D), F32, kind="Internal").ap()
        qd = nc.dram_tensor("qd", ((GROUPS + 1) * 2 * L, P), F32, kind="Internal").ap()
        kd = nc.dram_tensor("kd", ((GROUPS + 2) * L, ST), F32, kind="Internal").ap()
        vd = nc.dram_tensor("vd", ((GROUPS + 1) * L, DV), F32, kind="Internal").ap()
        cd = nc.dram_tensor("cd", ((UNITS + 1) * P, QH), F32, kind="Internal").ap()

        cst = sb("cst", [P, C_ALL])
        zero = sb("zero", [P, D])
        ones = sb("ones", [P, P])
        bias = sb("bias", [P, D])
        ident = cst[:, C_ID:C_ID + P]
        tri = cst[:, C_TRI:C_TRI + P]
        cosT = cst[:, C_COS:C_COS + TB * DK].rearrange("p (t d) -> p t d", d=DK)
        sinT = cst[:, C_SIN:C_SIN + TB * DK].rearrange("p (t d) -> p t d", d=DK)
        tie = cst[:, C_TIE:C_TIE + E * E].rearrange("p (e f) -> p e f", f=E)
        big = sb("big", [P, (E + 1) * (KC * 2 * I + IC * D)])
        n_gu = (E + 1) * KC * 2 * I
        w_gu = big[:, 0:n_gu]
        w_dn = big[:, n_gu:n_gu + (E + 1) * IC * D]
        GU, DN = KC * 2 * I, IC * D
        probs = big[:, 0:8 * 2 * QH].rearrange("p (k h q) -> p k h q", k=8, h=2)
        acc = big[:, 8192:12288].rearrange("p (u a h q) -> p u a h q", u=2, a=2, h=2)
        ctx_raw = big[:, 12288:13312].rearrange("p (r q) -> p r q", r=2)
        ctx_nrm = big[:, 13312:14336].rearrange("p (r q) -> p r q", r=2)
        den = big[:, 14336:14848]
        rden = big[:, 14848:15360]
        y_pick = big[:, 15360:15360 + NT * 2 * D].rearrange("p (t s d) -> p t s d", t=NT, s=2)
        ct = big[:, 23552:27648].rearrange("p (r c q) -> p r c q", r=4, c=8)
        mid = sb("mid", [P, 4608])
        xs = mid[:, 0:NT * D].rearrange("p (t d) -> p t d", d=D)
        q_nat = mid[:, 0:4 * QT * P].rearrange("p (r t c) -> p r t c", r=4, t=QT)
        k_nat = mid[:, 2048:2048 + TB * 3 * ST].rearrange("p (t c) -> p t c", t=TB)
        v_nat = mid[:, 3584:3584 + 2 * TB * DV].rearrange("p (r t d) -> p r t d", r=2, t=TB)
        KT = sb("KT", [P, 2, 2, L], F32R)
        QT1 = sb("QT1", [P, 2, QH], F32R)
        QT2 = sb("QT2", [P, 2, QH], F32R)
        w_in = sb("w_in", [P, KC, QK_COLS + VG_COLS])
        wrk = sb("wrk", [P, 2 * (NHK * ST + NKV * DV + 3 * QK_COLS)])
        stack = wrk[:, 0:2560].rearrange("p (r h c) -> p r h c", r=2, h=NHK)
        v_out = wrk[:, 2560:3072].rearrange("p (r c) -> p r c", r=2)
        rope_a = wrk[:, 3072:3712].rearrange("p (r h c) -> p r h c", r=2, h=NHK)
        rope_b = wrk[:, 3712:4352].rearrange("p (r h c) -> p r h c", r=2, h=NHK)
        roped = wrk[:, 4352:4992].rearrange("p (r h c) -> p r h c", r=2, h=NHK)
        gate_t = wrk[:, 0:1024].rearrange("p (r c) -> p r c", r=2)
        gate_s = wrk[:, 1024:2048].rearrange("p (r c) -> p r c", r=2)
        hid = wrk[:, 2048:3072].rearrange("p (r c) -> p r c", r=2)
        hidT = wrk[:, 3072:4096].rearrange("p (r c) -> p r c", r=2)
        y_sb = wrk[:, 4096:4608].rearrange("p (r c) -> p r c", r=2)
        wo = wrk[:, 0:8 * D].rearrange("p (c d) -> p c d", c=8)
        fx = wrk[:, 2048:2048 + 2 * D].rearrange("p (r d) -> p r d", r=2)
        fy = wrk[:, 2560:2560 + 2 * D].rearrange("p (r d) -> p r d", r=2)
        fa = wrk[:, 3072:3072 + 2 * D].rearrange("p (r d) -> p r d", r=2)
        fb = wrk[:, 3584:3584 + 2 * D].rearrange("p (r d) -> p r d", r=2)
        xt_in = sb("xt_in", [P, 2, D])
        xT = sb("xT", [P, 2, D])
        stats = sb("stats", [P, NT, 6])
        mv = sb("mv", [P, NT, 2])
        veps = sb("veps", [P, NT])
        std = sb("std", [P, NT])
        rstd = sb("rstd", [P, NT])
        mpart = sb("mpart", [P, 2, QT * 2 * 2])
        lg = sb("lg", [P, NT, E])
        r_gt = sb("r_gt", [P, NT * E * E])
        r_eq = sb("r_eq", [P, NT * E * E])
        rank = sb("rank", [P, NT, E])
        sel = sb("sel", [P, 3, NT, E])
        tmp = sb("tmp", [P, NT, E])
        best = sb("best", [P, 2, NT])
        wts = sb("wts", [P, 4, NT])
        cum = sb("cum", [P, 2, 8 + NT, E])
        cumt = sb("cumt", [P, 2, 4 + E])
        ntl = sb("ntl", [P, E])
        slotf = sb("slotf", [P, NT, E])
        posf = sb("posf", [P, 2, NT])
        pos = sb("pos", [P, 2, NT], I32)
        etf = sb("etf", [P, XTILES])
        etab = sb("etab", [P, 2 + XTILES], I32)

        ps_s = [ctx.enter_context(nc.psum_tensor(f"ps_s{i}", [P, 2 * 512], F32)) for i in range(2)]
        ps = [ctx.enter_context(nc.psum_tensor(f"ps{i}", [P, 512], F32)) for i in range(4, 8)]
        bank = [ps_s[0][:, 0:512], ps_s[0][:, 512:1024], ps_s[1][:, 0:512], ps_s[1][:, 512:1024]] + [p[:, :] for p in ps]
        ps_pass1, ps_ctx, ps_misc = bank[4:6], bank[6], bank[7]

        s_cst, s_win, s_wbase, s_wexp, s_bias = sem("cst_in"), sem("w_in_in"), sem("w_base_in"), sem("w_experts_in"), sem("bias_in")
        s_x = [sem(f"x_in{i}") for i in range(4)]
        s_mem = sem("constants_set")
        s_zero = sem("scratch_zeroed")
        s_bn, s_mv, s_veps, s_std, s_rstd = sem("bn_done"), sem("mv_done"), sem("veps_done"), sem("std_done"), sem("rstd_done")
        a_xn = sem("a_xn_ready")
        s_xd = sem("a_xn_in_dram")
        a_xl = sem("a_xn_tile")
        a_xtp, a_xt = sem("a_xT_in_psum"), sem("a_xT_ready")
        a_qk, a_vg = sem("a_qk_in_psum"), sem("a_vg_in_psum")
        a_vev = sem("a_v_evacuated")
        a_ra, a_rb = sem("a_rope_cos"), sem("a_rope_sin")
        a_ro, a_hi, a_lo = sem("a_roped"), sem("a_high_part"), sem("a_low_part")
        a_qst = [sem(f"a_qkv_stored{i}") for i in range(2)]
        r_ch, r_sel, r_cnt, r_d, r_e, r_pos = sem("r_chain"), sem("r_selected"), sem("r_counted"), sem("r_diff"), sem("r_exp"), sem("r_pos_ready")
        s_disp = sem("rows_dispatched")
        f_xl = [sem(f"f_x_loaded{i}") for i in range(2)]
        f_xtp, f_xt = sem("f_xT_in_psum"), sem("f_xT_ready")
        f_g, f_u, f_th, f_s, f_h = sem("f_gate_in_psum"), sem("f_up_in_psum"), sem("f_tanh"), sem("f_gate_silu"), sem("f_hidden")
        f_htp, f_ht, f_y, f_ye = sem("f_hT_in_psum"), sem("f_hT_ready"), sem("f_y_in_psum"), sem("f_y_evacuated")
        f_ys = [sem(f"f_y_stored{i}") for i in range(2)]
        t_q = [sem(f"t_q_loaded{i}") for i in range(4)]
        t_k, t_v = sem("t_k_loaded"), [sem(f"t_v_loaded{i}") for i in range(2)]
        t_kpad = sem("t_k_padding")
        t_misc, t_miscev = sem("t_misc_in_psum"), sem("t_misc_evacuated")
        t_p1, t_red, t_negm = sem("t_pass1_in_psum"), sem("t_pass1_reduced"), sem("t_negmax_ready")
        t_s, t_e, t_pv = sem("t_scores_in_psum"), sem("t_exp_done"), sem("t_pv_done")
        t_add, t_sum, t_cev = sem("t_probs_added"), sem("t_probs_summed"), sem("t_ctx_evacuated")
        t_rd, t_nrm = sem("t_den_inverted"), sem("t_ctx_normalised")
        t_cst = [sem(f"t_ctx_stored{i}") for i in range(2)]
        t_set = sem("t_standin_set")
        o_w = sem("o_w_in")
        o_in = [sem(f"o_tile_in{i}") for i in range(2)]
        o_ct = [sem(f"o_ctx_in{i}") for i in range(4)]
        o_y = [sem(f"o_rows_picked{i}") for i in range(4)]
        o_mm, o_f, o_done = sem("o_in_psum"), sem("o_chain"), sem("o_ready")
        o_st = [sem(f"o_stored{i}") for i in range(2)]

        PRO = [(-3, "T1"), (-3, "K0"), (-3, "K1"), (-3, "K2"), (-3, "K3"), (-2, "T1"), (-1, "T1"), (-1, "T2")]
        SLOT = {"T1": 0, "K0": 1, "K2": 1, "T2": 3, "DEN": 4, "K1": 6, "K3": 6}
        BODY = []
        for lu in range(8):
            k = {0: ["K0", "K1"], 1: ["K2", "K3"]}.get(lu % 4, [])
            BODY += [(lu, n) for n in sorted(["T1", "T2", "DEN"] + k, key=lambda n: SLOT[n])]

        def misc_index(it, lu, name):
            if it is None:
                return PRO.index((lu, name)) if lu < 0 else len(PRO) + 4 * len(BODY)
            return it * len(BODY) + (len(PRO) + BODY.index((lu, name)))

        def before_unit(it, lu):
            if it is None:
                return {-2: 5, -1: 6}[lu]
            if lu == 0:
                return it * len(BODY) + len(PRO)
            return misc_index(it, lu - 1, "K3" if lu % 4 == 2 else "T2") + 1

        def misc_of(lu, kt):
            return [n for l, n in BODY if l == lu and SLOT[n] == kt]

        def at(it, lu, per, plus=0):
            return per * lu + plus if it is None else it * (8 * per) + (per * lu + plus)

        block = ctx.enter_context(nc.Block())

        @block.sync
        def _(sp):
            sp.dma_start(cst[:, :], consts).then_inc(s_cst, 16)
            xv = x.rearrange("b (t p) d -> p (b t) d", p=P)
            for j in range(4):
                sp.dma_start(xs[:, 4 * j:4 * j + 4, :], xv[:, 4 * j:4 * j + 4, :]).then_inc(s_x[j], 16)
            sp.dma_start(w_in[:, :, 0:QK_COLS + NKV * DV], w_attn.rearrange("(k p) n -> p k n", p=P)).then_inc(s_win, 16)
            sp.dma_start(w_in[:, :, QK_COLS + NKV * DV:], gate_w.rearrange("(k p) n -> p k n", p=P)).then_inc(s_win, 16)
            for b in range(B):
                qb = qd[b * PAIRS * L:(b + 1) * PAIRS * L, :].rearrange("(c t) e -> t c e", c=PAIRS)
                kb = kd[b * NKV * L:(b + 1) * NKV * L, :].rearrange("(c t) e -> t c e", c=NKV)
                vb = vd[b * NKV * L:(b + 1) * NKV * L, :].rearrange("(c t) e -> t c e", c=NKV)
                with sp.Fori(0, TB // 2) as i:
                    for h in range(2):
                        t = i * 2 + (b * TB + h)
                        row = i * (2 * P) + h * P
                        sp.wait_ge(a_vev, t + 1)
                        sp.dma_start(vb[ds(row, P), :, :], v_out[:, h, :].rearrange("p (c d) -> p c d", c=NKV)).then_inc(a_qst[h], 16)
                        sp.wait_ge(a_lo, 2 * t + 2)
                        sp.dma_start(qb[ds(row, P), :, :], stack[:, h, 0:NH, :].rearrange("p (c e) k -> p c (e k)", c=PAIRS)).then_inc(a_qst[h], 16)
                        sp.dma_start(kb[ds(row, P), :, :], stack[:, h, NH:NHK, :]).then_inc(a_qst[h], 16)
            sp.dma_start(xd[0:TOK, :].rearrange("(t p) d -> p t d", p=P), xs[:, :, :]).then_inc(s_xd, 16)
            sp.dma_start(bias[:, :], b_out.partition_broadcast(P)).then_inc(s_bias, 16)

            def load_x(n, h):
                sp.wait_ge(f_xtp, n - 1)
                sp.dma_start(xt_in[:, h, :], xd[ds(n * P, P), :]).then_inc(f_xl[h], 16)

            def store_y(n, h):
                sp.wait_ge(f_ye, n + 1)
                sp.dma_start(yd[ds(n * P, P), :], y_sb[:, h, :]).then_inc(f_ys[h], 16)

            sp.wait_ge(a_xtp, NT)
            for n in range(2):
                sp.dma_start(xt_in[:, n, :], xs[:, n, :]).then_inc(f_xl[n], 16)
            sp.wait_ge(s_xd, 16)
            load_x(2, 0)
            with sp.Fori(0, (NT - 4) // 2) as i:
                for h in range(2):
                    n = i * 2 + (1 + h)
                    load_x(n + 2, (1 + h) % 2)
                    store_y(n - 1, h)
            load_x(NT - 1, 1)
            store_y(NT - 4, 0)
            sp.wait_ge(s_disp, 16 * 2 * NT)
            with sp.Fori(0, (NF - NT) // 2) as i:
                for h in range(2):
                    n = i * 2 + (NT - 2 + h)
                    load_x(n + 2, h)
                    store_y(n - 1, (1 + h) % 2)
            for n in (NF - 3, NF - 2, NF - 1):
                store_y(n, n % 2)

            def load_q(v, r):
                sp.dma_start(q_nat[:, r, :, :], qd[ds(v * QH, QH), :].rearrange("(t p) c -> p t c", p=P)).then_inc(t_q[r], 16)

            def load_k(g):
                sp.dma_start(k_nat[:, :, ST:2 * ST], kd[ds(g * L, L), :].rearrange("(t p) c -> p t c", p=P)).then_inc(t_k, 16)

            def load_v(g, r):
                sp.dma_start(v_nat[:, r, :, :], vd[ds(g * L, L), :].rearrange("(t p) c -> p t c", p=P)).then_inc(t_v[r], 16)

            for h in range(2):
                sp.wait_ge(a_qst[h], 16 + 48 * (NT // 2))
            sp.wait_ge(s_zero, 64)
            load_q(0, 0)
            load_k(0)
            for h in range(2):
                sp.wait_ge(f_ys[h], 16 + 16 * (NF // 2))
            sp.dma_start(wo, w_out.rearrange("(c p) d -> p c d", p=P)).then_inc(o_w, 16)
            for v in range(1, 4):
                load_q(v, v)
            load_v(0, 0)
            sp.wait_ge(t_misc, 5)
            load_k(1)
            with sp.Fori(0, UNITS // 8) as it:
                for lu in range(8):
                    sp.wait_ge(t_misc, before_unit(it, lu))
                    load_q(at(it, lu, 1, 4), lu % 4)
                    if lu % 4 == 0:
                        sp.wait_ge(t_pv, at(it, lu, 8, 8))
                        load_v(it * 2 + (lu // 4 + 1), (lu // 4 + 1) % 2)
                    if lu % 4 == 2:
                        sp.wait_ge(t_misc, misc_index(it, lu - 1, "K3") + 1)
                        load_k(it * 2 + (lu // 4 + 2))
                    sp.wait_ge(t_nrm, at(it, lu, 1, 3))
                    sp.dma_start(cd[ds(at(it, lu, 1) * P, P), :], ctx_nrm[:, (lu + 1) % 2, :]).then_inc(t_cst[(lu + 1) % 2], 16)
            xo = x.rearrange("b (t p) d -> (b t) p d", p=P)
            for t in range(NT):
                b, tb = divmod(t, TB)
                half, q0 = divmod(tb, QT)
                if t == 0:
                    for h in range(2):
                        sp.wait_ge(t_cst[h], 16 + 16 * (UNITS // 2))
                if t == TB:
                    sp.wait_ge(t_nrm, UNITS + 3)
                    sp.dma_start(cd[UNITS * P:(UNITS + 1) * P, :], ctx_nrm[:, 1, :]).then_inc(t_cst[1], 16)
                    sp.wait_ge(t_cst[1], 16 + 16 * (UNITS // 2 + 1))
                if t >= 4:
                    sp.wait_ge(o_mm, t - 3)
                src = cd[P * (1 + b * 16):P * (1 + (b + 1) * 16), :].rearrange("(c s p) q -> s p c q", s=2, p=P)
                sp.dma_start(ct[:, t % 4, :, :], src[half, :, :, q0 * P:(q0 + 1) * P]).then_inc(o_ct[t % 4], 16)
                if t >= 2:
                    sp.wait_ge(o_done, t - 1)
                sp.dma_start(fx[:, t % 2, :], xo[t]).then_inc(o_in[t % 2], 16)
                sp.dma_start(fy[:, t % 2, :], yd[t * P:(t + 1) * P, :]).then_inc(o_in[t % 2], 16)

        @block.gpsimd
        def _(pool):
            nc.gpsimd.memset(zero[:, :], 0.0).then_inc(s_mem, 1)
            nc.gpsimd.memset(ones[:, :], 1.0).then_inc(s_mem, 1)
            nc.gpsimd.memset(stack[:, :, :, MCOL:], 0.0).then_inc(s_mem, 1)
            pool.wait_ge(s_mem, 3)
            nc.gpsimd.memset(stack[:, :, NH:, MCOL:MCOL + 1], 1.0).then_inc(s_mem, 1)
            nc.gpsimd.memset(cum[:, :, :, :], 0.0).then_inc(s_mem, 1)
            nc.gpsimd.memset(cumt[:, :, :], 0.0).then_inc(s_mem, 1)
            nc.gpsimd.memset(etab[:, 0:2], E).then_inc(s_mem, 1)
            pool.wait_ge(s_mem, 7)
            pool.wait_ge(a_xn, NT)
            for t in range(2):
                nc.gpsimd.tensor_copy(xt_in[:, t, :], xs[:, t, :]).then_inc(a_xl, 1)
            for b in range(B):
                with pool.Fori(0, TB // 2 - b) as i:
                    for h in range(2):
                        t = i * 2 + (b * TB + h)
                        pool.wait_ge(a_xtp, t + 1)
                        nc.gpsimd.tensor_copy(xt_in[:, h:h + 1, :], xs[:, ds(t + 2, 1), :]).then_inc(a_xl, 1)
                        pool.wait_ge(a_hi, 2 * t + 2)
                        nc.gpsimd.tensor_tensor(stack[:, h, 0:NH, 2 * DK:3 * DK].bitcast(F32R), roped[:, h, 0:NH, :],
                                                stack[:, h, 0:NH, 0:DK], ALU.subtract).then_inc(a_lo, 1)
                        nc.gpsimd.tensor_tensor(stack[:, h, NH:, DK:2 * DK].bitcast(F32R), roped[:, h, NH:, :],
                                                stack[:, h, NH:, 0:DK], ALU.subtract).then_inc(a_lo, 1)
            for t in (NT - 2, NT - 1):
                h = t % 2
                pool.wait_ge(a_hi, 2 * t + 2)
                nc.gpsimd.tensor_tensor(stack[:, h, 0:NH, 2 * DK:3 * DK].bitcast(F32R), roped[:, h, 0:NH, :],
                                        stack[:, h, 0:NH, 0:DK], ALU.subtract).then_inc(a_lo, 1)
                nc.gpsimd.tensor_tensor(stack[:, h, NH:, DK:2 * DK].bitcast(F32R), roped[:, h, NH:, :],
                                        stack[:, h, NH:, 0:DK], ALU.subtract).then_inc(a_lo, 1)
            pool.wait_ge(s_zero, 64)
            pool.wait_ge(s_xd, 16)
            pool.wait_ge(r_pos, 2)
            for t in range(NT):
                for s in range(2):
                    pool.indirect_dma_start(xd, bass.IndirectOffsetOnAxis(ap=pos[:, s, t:t + 1], axis=0),
                                            xs[:, t, :], None).then_inc(s_disp, 16)
            pool.wait_ge(s_disp, 16 * 2 * NT)
            nc.gpsimd.memset(k_nat[:, :, 0:ST], 0.0).then_inc(t_kpad, 1)
            nc.gpsimd.memset(k_nat[:, :, 2 * ST:], 0.0).then_inc(t_kpad, 1)
            nc.gpsimd.memset(v_nat[:, 1, :, :], 0.0).then_inc(t_set, 1)
            pool.wait_ge(f_y, NF)
            nc.gpsimd.memset(probs[:, 0, :, :], 1.0).then_inc(t_set, 1)
            nc.gpsimd.memset(probs[:, 7, :, :], 1.0).then_inc(t_set, 1)
            nc.gpsimd.memset(acc[:, 1, :, :, :], 1.0).then_inc(t_set, 1)
            pool.sem_inc(t_add, 6)
            with pool.Fori(0, UNITS // 8) as it:
                for lu in range(8):
                    u2 = lu % 2
                    for a, (first, kt) in enumerate([(0, 1), (2, 3), (None, 4), (None, 5), (None, 6), (None, 7)]):
                        pool.wait_ge(t_e, at(it, lu, 8, kt + 3))
                        o = acc[:, u2, a % 2, :, :]
                        if first is None:
                            pool.wait_ge(t_add, at(it, lu, 6, 6 + a - 1))
                            nc.gpsimd.tensor_tensor(o, o, probs[:, kt, :, :], ALU.add).then_inc(t_add, 1)
                        else:
                            if a == 0:
                                if lu:
                                    pool.wait_ge(t_misc, misc_index(it, lu - 1, "DEN") + 1)
                                else:
                                    pool.wait_ge(t_misc, it * len(BODY) + len(PRO))
                            nc.gpsimd.tensor_tensor(o, probs[:, first, :, :], probs[:, kt, :, :], ALU.add).then_inc(t_add, 1)
            for h in range(2):
                pool.wait_ge(f_ys[h], 16 + 16 * (NF // 2))
            for t in range(NT):
                for s in range(2):
                    pool.indirect_dma_start(y_pick[:, t, s, :], None, yd,
                                            bass.IndirectOffsetOnAxis(ap=pos[:, s, t:t + 1], axis=0)).then_inc(o_y[t % 4], 16)
                if t >= 3:
                    pool.wait_ge(o_y[(t - 3) % 4], 32 * ((t - 3) // 4 + 1))

        @block.scalar
        def _(act):
            act.wait_ge(s_mem, 1)
            act.dma_start(xd[TOK:ROWS, :].rearrange("(k p) d -> p k d", p=P),
                          zero[:, :].unsqueeze(1).to_broadcast([P, XTILES, D])).then_inc(s_zero, 16)
            def load_weights(e):
                gu, dn = (base_gu, base_dn) if e == E else (exp_gu[e], exp_dn[e])
                act.dma_start(w_gu[:, e * GU:(e + 1) * GU].rearrange("p (k n) -> p k n", k=KC),
                              gu.rearrange("(k p) n -> p k n", p=P)).then_inc(s_wbase if e == E else s_wexp, 16)
                act.dma_start(w_dn[:, e * DN:(e + 1) * DN].rearrange("p (k n) -> p k n", k=IC),
                              dn.rearrange("(k p) n -> p k n", p=P)).then_inc(s_wbase if e == E else s_wexp, 16)

            load_weights(E)
            for h in range(2):
                act.sem_inc(a_qst[h], 16)
                act.sem_inc(f_ys[h], 16)
                act.sem_inc(t_cst[h], 16)
                act.sem_inc(o_st[h], 16)
            act.sem_inc(t_e, 2)
            act.sem_inc(t_pv, 6)
            act.sem_inc(t_nrm, 2)
            act.wait_ge(s_veps, 1)
            nc.scalar.activation(std[:, :], veps[:, :], ACT.Sqrt).then_inc(s_std, 1)
            act.sem_inc(a_vg, 2)
            act.sem_inc(a_ro, 2)

            def a_xT_out(t, h):
                act.wait_ge(a_xtp, t + 1)
                act.wait_ge(a_vg, t + 1)
                nc.scalar.activation(xT[:, h, :], bank[5 * h][:, 0:D], ACT.Copy).then_inc(a_xt, 1)

            def a_out(t, h, stored):
                act.wait_ge(a_vg, t + 3)
                act.wait_ge(a_qst[h], stored)
                nc.scalar.activation(v_out[:, h, :], bank[3 + h][:, 0:NKV * DV], ACT.Copy)
                nc.scalar.activation(lg[:, ds(t, 1), :], bank[3 + h][:, NKV * DV:VG_COLS].unsqueeze(1), ACT.Copy).then_inc(a_vev, 1)
                act.wait_ge(a_ro, t + 3)
                nc.scalar.activation(stack[:, h, 0:NH, 0:2 * DK].rearrange("p h (c k) -> p h c k", c=2).bitcast(F32R),
                                     roped[:, h, 0:NH, :].unsqueeze(2).to_broadcast([P, NH, 2, DK]), ACT.Copy).then_inc(a_hi, 1)
                nc.scalar.activation(stack[:, h, NH:, 0:4 * DK].rearrange("p h (c k) -> p h c k", c=2)[:, :, :, 0:DK].bitcast(F32R),
                                     roped[:, h, NH:, :].unsqueeze(2).to_broadcast([P, NKV, 2, DK]), ACT.Copy).then_inc(a_hi, 1)

            a_xT_out(0, 0)
            for b in range(B):
                with act.Fori(0, TB // 2 - b) as i:
                    for h in range(2):
                        t = i * 2 + (b * TB + h)
                        a_xT_out(t + 1, 1 - h)
                        a_out(t, h, i * 48 + (16 + 48 * 4 * b))
            a_xT_out(NT - 1, 1)
            a_out(NT - 2, 0, 16 + 48 * (NT // 2 - 1))
            a_out(NT - 1, 1, 16 + 48 * (NT // 2 - 1))
            for e in range(E):
                load_weights(e)
            act.dma_start(qd[GROUPS * 2 * L:, :].rearrange("(k p) d -> p k d", p=P),
                          zero[:, 0:P].unsqueeze(1).to_broadcast([P, 2 * L // P, P])).then_inc(s_zero, 16)
            act.dma_start(kd[GROUPS * L:, :].rearrange("(k p) d -> p k d", p=P),
                          zero[:, 0:ST].unsqueeze(1).to_broadcast([P, 2 * L // P, ST])).then_inc(s_zero, 16)
            act.dma_start(vd[GROUPS * L:, :].rearrange("(k p) d -> p k d", p=P),
                          zero[:, 0:DV].unsqueeze(1).to_broadcast([P, L // P, DV])).then_inc(s_zero, 16)
            for h in range(2):
                act.wait_ge(a_qst[h], 16 + 48 * (NT // 2))

            def ev_xT(n, h):
                act.wait_ge(f_xtp, n + 1)
                nc.scalar.activation(xT[:, h, :], bank[0][:, 0:D], ACT.Copy).then_inc(f_xt, 1)

            def tanh(n, h):
                act.wait_ge(f_g, n + 1)
                nc.scalar.activation(gate_t[:, h, :], bank[1 + 2 * h], ACT.Tanh, scale=0.5).then_inc(f_th, 1)

            def ev_hT(n, h):
                act.wait_ge(f_htp, n + 1)
                nc.scalar.activation(hidT[:, h, :], bank[5], ACT.Copy).then_inc(f_ht, 1)

            ev_xT(0, 0)
            tanh(0, 0)
            ev_xT(1, 1)

            def act_step(n, h):
                tanh(n, h)
                ev_hT(n - 1, 1 - h)
                act.wait_ge(f_u, n)
                ev_xT(n + 1, 1 - h)

            for n in range(1, 5):
                act_step(n, n % 2)
                if n == 3:
                    act.wait_ge(r_d, 1)
                    nc.scalar.activation(wts[:, 1, :], wts[:, 0, :], ACT.Exp).then_inc(r_e, 1)
            with act.Fori(0, (NF - 6) // 2) as i:
                for h in range(2):
                    act_step(i * 2 + (5 + h), 1 - h)
            tanh(NF - 1, 1)
            ev_hT(NF - 2, 0)
            ev_hT(NF - 1, 1)

            def ev_misc(it, lu, name):
                act.wait_ge(t_misc, misc_index(it, lu, name) + 1)
                if name == "T1":
                    dst = QT1[:, (lu + 3) % 2, :]
                elif name == "T2":
                    dst = QT2[:, (lu + 1) % 2, :]
                elif name == "DEN":
                    act.wait_ge(t_nrm, at(it, lu, 1, 2))
                    dst = den
                else:
                    g2 = 0 if lu < 0 else (lu // 4 + 1) % 2
                    k = int(name[1])
                    dst = KT[:, g2, k // 2, (k % 2) * 512:(k % 2 + 1) * 512]
                nc.scalar.activation(dst, ps_misc, ACT.Copy).then_inc(t_miscev, 1)

            ADDS = [1, 1, 2, 2, 3, 4, 5, 6]
            for lu, name in PRO:
                ev_misc(None, lu, name)
            with act.Fori(0, UNITS // 8) as it:
                for lu in range(8):
                    for kt in range(8):
                        act.wait_ge(t_s, at(it, lu, 8, kt + 1))
                        act.wait_ge(t_pv, at(it, lu, 8, kt + 1))
                        act.wait_ge(t_add, at(it, lu, 6, ADDS[kt]))
                        nc.scalar.activation(probs[:, kt, :, :], ps_s[kt % 2][:, :].rearrange("p (h q) -> p h q", h=2),
                                             ACT.Exp, scale=SCALE).then_inc(t_e, 1)
                        if kt == 0:
                            act.wait_ge(t_pv, at(it, lu, 8, 8))
                            act.wait_ge(t_nrm, at(it, lu, 1, 1))
                            nc.scalar.activation(ctx_raw[:, (lu + 1) % 2, :], ps_ctx, ACT.Copy).then_inc(t_cev, 1)
                        for name in misc_of(lu, kt):
                            ev_misc(it, lu, name)
            act.wait_ge(t_pv, 8 * UNITS + 8)
            act.wait_ge(t_nrm, UNITS + 1)
            nc.scalar.activation(ctx_raw[:, 1, :], ps_ctx, ACT.Copy).then_inc(t_cev, 1)
            act.wait_ge(t_misc, len(PRO) + 4 * len(BODY) + 1)
            act.wait_ge(t_nrm, UNITS + 2)
            nc.scalar.activation(den, ps_misc, ACT.Copy).then_inc(t_miscev, 1)

            ov = out.rearrange("b (t p) d -> (b t) p d", p=P)
            for t in range(NT):
                act.wait_ge(o_done, t + 1)
                act.dma_start(ov[t], fb[:, t % 2, :]).then_inc(o_st[t % 2], 16)
            for h in range(2):
                act.wait_ge(o_st[h], 16 + 16 * (NT // 2))

        @block.vector
        def _(dve):
            for t in range(NT):
                if t % 4 == 0:
                    dve.wait_ge(s_x[t // 4], 16)
                nc.vector.bn_stats(stats[:, t, :], xs[:, t, :]).then_inc(s_bn, 1)
            for t in range(NT):
                dve.wait_ge(s_bn, t + 1)
                nc.vector.bn_aggr(mv[:, t, :], stats[:, t, :]).then_inc(s_mv, 1)
            dve.wait_ge(s_mv, NT)
            nc.vector.tensor_scalar(veps[:, :], mv[:, :, 1], EPS, None, ALU.add).then_inc(s_veps, 1)
            dve.wait_ge(s_std, 1)
            nc.vector.reciprocal(rstd[:, :], std[:, :]).then_inc(s_rstd, 1)
            dve.wait_ge(s_rstd, 1)
            dve.wait_ge(s_cst, 16)
            for t in range(NT):
                nc.vector.tensor_scalar(xs[:, t, :], xs[:, t, :], mv[:, t, 0:1], rstd[:, t:t + 1],
                                        ALU.subtract, ALU.mult).then_inc(a_xn, 1)
            for b in range(B):
                with dve.Fori(0, TB // 2) as i:
                    for h in range(2):
                        t = i * 2 + (b * TB + h)
                        dve.wait_ge(a_qk, t + 1)
                        qk = bank[1 + h][:, 0:QK_COLS].rearrange("p (h c) -> p h c", c=DK)
                        tb = i * 2 + h
                        H2 = DK // 2
                        cs = cosT[:, ds(tb, 1), :].to_broadcast([P, NHK, DK])
                        sn = sinT[:, ds(tb, 1), :].to_broadcast([P, NHK, DK])
                        nc.vector.tensor_tensor(rope_a[:, h, :, :], qk, cs, ALU.mult).then_inc(a_ra, 1)
                        nc.vector.tensor_tensor(rope_b[:, h, :, 0:H2], qk[:, :, H2:], sn[:, :, 0:H2], ALU.mult).then_inc(a_rb, 1)
                        nc.vector.tensor_tensor(rope_b[:, h, :, H2:], qk[:, :, 0:H2], sn[:, :, H2:], ALU.mult).then_inc(a_rb, 1)
                        dve.wait_ge(a_ra, t + 1)
                        dve.wait_ge(a_rb, 2 * t + 2)
                        dve.wait_ge(a_qst[h], i * 48 + (16 + 48 * 4 * b))
                        nc.vector.tensor_tensor(roped[:, h, :, :], rope_a[:, h, :, :], rope_b[:, h, :, :], ALU.add).then_inc(a_ro, 1)

            def gate(n, h):
                dve.wait_ge(f_th, n + 1)
                V.scalar_tensor_tensor(gate_s[:, h, :], gate_t[:, h, :], 1.0, bank[1 + 2 * h], ALU.add, ALU.mult).then_inc(f_s, 1)
                dve.wait_ge(f_s, n + 1)
                dve.wait_ge(f_u, n + 1)
                V.scalar_tensor_tensor(hid[:, h, :], gate_s[:, h, :], 0.5, bank[2 + 2 * h], ALU.mult, ALU.mult).then_inc(f_h, 1)

            def ev_y(n, h):
                dve.wait_ge(f_y, n + 1)
                V.tensor_copy(y_sb[:, h, :], bank[6][:, 0:D]).then_inc(f_ye, 1)

            steps = [0]

            def link(ins):
                steps[0] += 1
                ins.then_inc(r_ch, 1)
                dve.wait_ge(r_ch, steps[0])

            dve.wait_ge(a_vev, NT)
            dve.wait_ge(s_mem, 7)
            V = nc.vector
            full = [P, NT, E, E]
            pre = bank[7][:, 0:NT * E].rearrange("p (t e) -> p t e", e=E)
            tot = bank[7][:, NT * E:2 * NT * E].rearrange("p (t e) -> p t e", e=E)
            c_end, x_end = 0, 1
            gt4 = r_gt[:, :].rearrange("p (t e f) -> p t e f", e=E, f=E)
            eq4 = r_eq[:, :].rearrange("p (t e f) -> p t e f", e=E, f=E)
            l_f = lg[:, :, :].unsqueeze(2).to_broadcast(full)
            l_e = lg[:, :, :].unsqueeze(3).to_broadcast(full)
            def route_rank():
                link(V.tensor_tensor(gt4, l_f, l_e, ALU.is_gt))
                link(V.tensor_tensor(eq4, l_f, l_e, ALU.is_equal))
                link(V.tensor_tensor(eq4, eq4, tie.unsqueeze(1).to_broadcast(full), ALU.mult))

            def route_rank2():
                link(V.tensor_tensor(r_gt[:, :], r_gt[:, :], r_eq[:, :], ALU.add))
                link(V.tensor_reduce(rank[:, :, :], gt4, AX.X, ALU.add))

            def route_select():
                for s in range(2):
                    link(V.tensor_scalar(sel[:, s, :, :], rank[:, :, :], float(s), None, ALU.is_equal))
                    link(V.tensor_tensor(tmp[:, :, :], sel[:, s, :, :], lg[:, :, :], ALU.mult))
                    link(V.tensor_reduce(best[:, s, :], tmp[:, :, :], AX.X, ALU.add))
                V.tensor_tensor(sel[:, 2, :, :], sel[:, 0, :, :], sel[:, 1, :, :], ALU.add).then_inc(r_sel, 1)
                V.tensor_tensor(wts[:, 0, :], best[:, 1, :], best[:, 0, :], ALU.subtract).then_inc(r_d, 1)

            def route_weights():
                dve.wait_ge(r_e, 1)
                link(V.tensor_scalar(wts[:, 3, :], wts[:, 1, :], 1.0, None, ALU.add))
                link(V.reciprocal(wts[:, 2, :], wts[:, 3, :]))
                link(V.tensor_tensor(wts[:, 3, :], wts[:, 1, :], wts[:, 2, :], ALU.mult))

            def route_counts():
                dve.wait_ge(r_cnt, 1)
                link(V.tensor_copy(tmp[:, :, :], tot))
                link(V.tensor_copy(cum[:, 0, 8:, :], tmp[:, :, :]))
                src = 0
                for sh in (1, 2, 4, 8):
                    link(V.tensor_tensor(cum[:, 1 - src, 8:, :], cum[:, src, 8:, :], cum[:, src, 8 - sh:8 + NT - sh, :], ALU.add))
                    src = 1 - src

            def route_tiles():
                thr = cst[:, C_THR:C_THR + NT].unsqueeze(1).to_broadcast([P, E, NT])
                cmp = r_gt[:, 0:E * NT].rearrange("p (e k) -> p e k", e=E)
                cnt = cum[:, c_end, 8 + NT - 1, :].unsqueeze(2).to_broadcast([P, E, NT])
                link(V.tensor_tensor(cmp, cnt, thr, ALU.is_gt))
                link(V.tensor_reduce(ntl[:, :], cmp, AX.X, ALU.add))
                link(V.tensor_copy(cumt[:, 0, 4:], ntl[:, :]))
                s2 = 0
                for sh in (1, 2, 4):
                    link(V.tensor_tensor(cumt[:, 1 - s2, 4:], cumt[:, s2, 4:], cumt[:, s2, 4 - sh:4 + E - sh], ALU.add))
                    s2 = 1 - s2

            def route_experts():
                cm2 = r_eq[:, 0:XTILES * E].rearrange("p (k e) -> p k e", e=E)
                link(V.tensor_tensor(cm2, cumt[:, x_end, 4:].unsqueeze(1).to_broadcast([P, XTILES, E]),
                                     cst[:, C_TIX:C_TIX + XTILES].unsqueeze(2).to_broadcast([P, XTILES, E]), ALU.is_le))
                link(V.tensor_reduce(etf[:, :], cm2, AX.X, ALU.add))
                link(V.tensor_scalar(etab[:, 2:], etf[:, :], float(E - 1), None, ALU.min))

            def route_slots():
                link(V.tensor_tensor(ntl[:, :], cumt[:, x_end, 4:], ntl[:, :], ALU.subtract))
                link(V.tensor_scalar(ntl[:, :], ntl[:, :], float(P), float(TOK), ALU.mult, ALU.add))
                link(V.tensor_tensor(slotf[:, :, :], cum[:, c_end, 8:, :], tmp[:, :, :], ALU.subtract))
                link(V.tensor_tensor(slotf[:, :, :], slotf[:, :, :], pre, ALU.add))
                link(V.tensor_tensor(slotf[:, :, :], slotf[:, :, :], ntl[:, :].unsqueeze(1).to_broadcast([P, NT, E]), ALU.add))

            def route_positions():
                for s in range(2):
                    link(V.tensor_tensor(tmp[:, :, :], sel[:, s, :, :], slotf[:, :, :], ALU.mult))
                    link(V.tensor_reduce(posf[:, s, :], tmp[:, :, :], AX.X, ALU.add))
                    V.tensor_copy(pos[:, s, :], posf[:, s, :]).then_inc(r_pos, 1)

            between = [route_rank, route_rank2, route_select, route_weights, route_counts, route_tiles, route_experts,
                       route_slots, route_positions]
            for n, part in enumerate(between):
                gate(n, n % 2)
                if n:
                    dve.wait_ge(f_ys[(n - 1) % 2], (n - 1) // 2 * 16 + 16)
                    ev_y(n - 1, (n - 1) % 2)
                part()
            n0 = len(between)
            with dve.Fori(0, (NF - 1 - n0) // 2) as i:
                for h in range(2):
                    n = i * 2 + (n0 + h)
                    gate(n, (n0 + h) % 2)
                    dve.wait_ge(f_ys[(n0 + h - 1) % 2], i * 16 + ((n0 + h - 1) // 2 * 16 + 16))
                    ev_y(n - 1, (n0 + h - 1) % 2)
            gate(NF - 1, 1)
            dve.wait_ge(f_ys[0], 16 * ((NF - 2) // 2 + 1))
            ev_y(NF - 2, 0)
            dve.wait_ge(f_ys[1], 16 * ((NF - 2) // 2 + 1))
            ev_y(NF - 1, 1)

            def reduce(it, lu, j):
                dve.wait_ge(t_p1, at(it, lu + 2, 16, j + 1))
                V.tensor_reduce(mpart[:, lu % 2, j:j + 1], ps_pass1[j % 2], AX.X, ALU.max).then_inc(t_red, 1)

            def negmax(it, lu):
                dve.wait_ge(t_red, at(it, lu + 2, 16, 16))
                V.tensor_reduce(q_nat[:, (lu + 2) % 4, :, :].rearrange("p t (e c) -> p t e c", e=2)[:, :, :, MCOL].bitcast(F32R),
                                mpart[:, lu % 2, :].rearrange("p (t e k) -> p t e k", e=2, k=2),
                                AX.X, ALU.max, negate=True).then_inc(t_negm, 1)

            def invert(it, lu, c):
                if c == 0:
                    dve.wait_ge(t_miscev, misc_index(it, lu, "DEN") + 1)
                V.reciprocal(rden[:, c * P:(c + 1) * P], den[:, c * P:(c + 1) * P]).then_inc(t_rd, 1)

            def normalise(it, lu):
                dve.wait_ge(t_rd, at(it, lu, 4, 4))
                dve.wait_ge(t_cev, at(it, lu, 1, 1))
                dve.wait_ge(t_cst[(lu + 1) % 2], 16 * (lu // 2) + 16 if it is None else it * 64 + (16 * (lu // 2) + 16))
                V.tensor_tensor(ctx_nrm[:, (lu + 1) % 2, :], ctx_raw[:, (lu + 1) % 2, :], rden, ALU.mult).then_inc(t_nrm, 1)

            def total(it, lu):
                dve.wait_ge(t_add, at(it, lu, 6, 6))
                a = acc[:, (lu - 1) % 2, :, :, :]
                V.tensor_tensor(a[:, 0, :, :], a[:, 0, :, :], a[:, 1, :, :], ALU.add).then_inc(t_sum, 1)

            for lu in (-2, -1):
                for j in range(16):
                    reduce(None, lu, j)
                negmax(None, lu)
            dve.wait_ge(t_set, 4)
            with dve.Fori(0, UNITS // 8) as it:
                for lu in range(8):
                    for kt in range(8):
                        reduce(it, lu, 2 * kt)
                        reduce(it, lu, 2 * kt + 1)
                        if kt == 3:
                            total(it, lu)
                        if kt >= 5:
                            invert(it, lu, kt - 5)
                    negmax(it, lu)
                    invert(it, lu, 3)
                    normalise(it, lu)
            total(None, UNITS)
            for c in range(4):
                invert(None, UNITS, c)
            normalise(None, UNITS)

            f = [0]

            def olink(ins):
                f[0] += 1
                ins.then_inc(o_f, 1)
                dve.wait_ge(o_f, f[0])

            dve.wait_ge(s_bias, 16)
            for t in range(NT):
                h = t % 2
                dve.wait_ge(o_in[h], 32 * (t // 2 + 1))
                olink(V.tensor_tensor(fa[:, h, :], fx[:, h, :], fy[:, h, :], ALU.add))
                olink(V.tensor_tensor(fa[:, h, :], fa[:, h, :], bias[:, :], ALU.add))
                dve.wait_ge(o_y[t % 4], 32 * (t // 4 + 1))
                olink(V.scalar_tensor_tensor(fa[:, h, :], y_pick[:, t, 0, :], wts[:, 2, t:t + 1], fa[:, h, :], ALU.mult, ALU.add))
                olink(V.scalar_tensor_tensor(fa[:, h, :], y_pick[:, t, 1, :], wts[:, 3, t:t + 1], fa[:, h, :], ALU.mult, ALU.add))
                dve.wait_ge(o_mm, t + 1)
                dve.wait_ge(o_st[h], 16 * (t // 2 + 1))
                V.tensor_tensor(fb[:, h, :], fa[:, h, :], bank[h][:, 0:D], ALU.add).then_inc(o_done, 1)

        @block.tensor
        def _(pe):
            mm = nc.tensor.matmul
            tr = nc.tensor.transpose
            pe.wait_ge(s_cst, 16)
            pe.wait_ge(s_win, 32)

            def a_xT_in(t, h):
                pe.wait_ge(a_xl, t + 1)
                for k in range(KC):
                    last = tr(bank[5 * h][:, k * P:(k + 1) * P], xt_in[:, h, k * P:(k + 1) * P], ident)
                last.then_inc(a_xtp, 1)

            def a_project(t, h):
                pe.wait_ge(a_xt, t + 1)
                pe.wait_ge(a_ro, t + 1)
                for k in range(KC):
                    last = mm(bank[1 + h][:, 0:QK_COLS], xT[:, h, k * P:(k + 1) * P], w_in[:, k, 0:QK_COLS],
                              start=k == 0, stop=k == KC - 1)
                last.then_inc(a_qk, 1)
                for k in range(KC):
                    last = mm(bank[3 + h][:, 0:VG_COLS], xT[:, h, k * P:(k + 1) * P], w_in[:, k, QK_COLS:],
                              start=k == 0, stop=k == KC - 1)
                last.then_inc(a_vg, 1)

            a_xT_in(0, 0)
            for b in range(B):
                with pe.Fori(0, TB // 2 - b) as i:
                    for h in range(2):
                        t = i * 2 + (b * TB + h)
                        a_xT_in(t + 1, 1 - h)
                        a_project(t, h)
            a_xT_in(NT - 1, 1)
            a_project(NT - 2, 0)
            a_project(NT - 1, 1)

            pe.wait_ge(a_ro, NT + 2)
            pe.wait_ge(a_vev, NT)
            pe.wait_ge(s_wbase, 32)

            def x_T(n, h, l):
                pe.wait_ge(f_xl[h], l)
                pe.wait_ge(f_xt, n)
                for k in range(KC):
                    last = tr(bank[0][:, k * P:(k + 1) * P], xt_in[:, h, k * P:(k + 1) * P], ident)
                last.then_inc(f_xtp, 1)

            def up(n, h, half, e):
                for k in range(KC):
                    last = mm(bank[1 + 2 * h + half], xT[:, h, k * P:(k + 1) * P],
                              w_gu[:, ds(e * GU + (k * 2 * I + half * I), I)], start=k == 0, stop=k == KC - 1)
                last.then_inc((f_g, f_u)[half], 1)

            def h_T(n, h):
                pe.wait_ge(f_h, n + 1)
                for k in range(IC):
                    last = tr(bank[5][:, k * P:(k + 1) * P], hid[:, h, k * P:(k + 1) * P], ident)
                last.then_inc(f_htp, 1)

            def down(n, h, e):
                pe.wait_ge(f_ht, n + 1)
                for k in range(IC):
                    last = mm(bank[6][:, 0:D], hidT[:, h, k * P:(k + 1) * P], w_dn[:, ds(e * DN + k * D, D)],
                              start=k == 0, stop=k == IC - 1)
                last.then_inc(f_y, 1)

            def step(n, h, xl, e, e_before):
                pe.wait_ge(f_xt, n + 1)
                up(n, h, 0, e)
                h_T(n - 1, 1 - h)
                up(n, h, 1, e)
                x_T(n + 1, 1 - h, xl)
                pe.wait_ge(f_ye, n - 1) if not isinstance(n, int) or n > 1 else None
                down(n - 1, 1 - h, e_before)

            pe.wait_ge(f_xl[0], 16)
            for k in range(KC):
                last = tr(bank[0][:, k * P:(k + 1) * P], xt_in[:, 0, k * P:(k + 1) * P], ident)
            last.then_inc(f_xtp, 1)
            pe.wait_ge(f_xt, 1)
            up(0, 0, 0, E)
            up(0, 0, 1, E)
            x_T(1, 1, 16)
            for n in range(1, 5):
                step(n, n % 2, 16 * ((n + 1) // 2 + 1), E, E)
            pe.wait_ge(r_sel, 1)
            pe.wait_ge(s_mem, 2)
            sflat = sel[:, 2, :, :].rearrange("p t e -> p (t e)")
            mm(bank[7][:, 0:NT * E], tri, sflat, start=True, stop=True)
            mm(bank[7][:, NT * E:2 * NT * E], ones[:, :], sflat, start=True, stop=True).then_inc(r_cnt, 1)
            with pe.Fori(0, (NT - 6) // 2) as i:
                for h in range(2):
                    step(i * 2 + (5 + h), 1 - h, i * 16 + 64, E, E)
            pe.wait_ge(s_wexp, 16 * 2 * E)
            pe.wait_ge(r_pos, 2)
            with pe.Fori(0, (NF - NT) // 2) as i:
                for h in range(2):
                    e0 = pe.value_load(etab[0:1, ds(i * 2 + h, 1)], min_val=0, max_val=E)
                    e1 = pe.value_load(etab[0:1, ds(i * 2 + (h + 1), 1)], min_val=0, max_val=E)
                    step(i * 2 + (NT - 1 + h), 1 - h, i * 16 + 16 * (NT // 2 + 1), e1, e0)
            e0 = pe.value_load(etab[0:1, XTILES:XTILES + 1], min_val=0, max_val=E)
            e1 = pe.value_load(etab[0:1, XTILES + 1:XTILES + 2], min_val=0, max_val=E)
            n = NF - 1
            pe.wait_ge(f_xt, NF)
            up(n, 1, 0, e1)
            h_T(n - 1, 0)
            up(n, 1, 1, e1)
            pe.wait_ge(f_ye, n - 1)
            down(n - 1, 0, e0)
            pe.wait_ge(f_ht, NF - 1)
            h_T(n, 1)
            pe.wait_ge(f_ye, n)
            down(n, 1, e1)

            def misc(it, lu, name):
                pe.wait_ge(t_miscev, misc_index(it, lu, name)) if not (it is None and (lu, name) == PRO[0]) else None
                if name == "T1":
                    v = lu + 3
                    cnt = v // 4 * 16 + 16 if it is None else it * 32 + (v // 4 * 16 + 16)
                    pe.wait_ge(t_q[v % 4], cnt)
                    for j in range(QT):
                        last = tr(ps_misc[:, j * P:(j + 1) * P], q_nat[:, v % 4, j, :], ident)
                elif name == "T2":
                    v = lu + 1
                    pe.wait_ge(t_negm, at(it, v, 1, 1))
                    for j in range(QT):
                        last = tr(ps_misc[:, j * P:(j + 1) * P], q_nat[:, v % 4, j, :], ident)
                elif name == "DEN":
                    pe.wait_ge(t_sum, at(it, lu, 1, 1))
                    for e in range(2):
                        last = mm(ps_misc[e * DV:(e + 1) * DV, :], ones[:, 0:DV], acc[:, (lu - 1) % 2, 0, e, :],
                                  start=True, stop=True)
                else:
                    k = int(name[1])
                    g1 = 16 if it is None else it * 32 + (lu // 4 * 16 + 32)
                    pe.wait_ge(t_k, g1)
                    var = k // 2
                    c0 = ST * (1 - var)
                    for j in range(QT):
                        last = tr(ps_misc[:, j * P:(j + 1) * P], k_nat[:, (k % 2) * QT + j, c0:c0 + P], ident)
                last.then_inc(t_misc, 1)

            def fill(it, lu, j):
                qt, e, kc = j // 4, j // 2 % 2, j % 2
                if not (it is None and lu == -2 and j < 2):
                    pe.wait_ge(t_red, at(it, lu + 2, 16, j - 1))
                if j == 0:
                    pe.wait_ge(t_miscev, before_unit(it, lu))
                g2 = (lu + 2) // 4 % 2
                mm(ps_pass1[j % 2], QT1[:, lu % 2, qt * P:(qt + 1) * P], KT[:, g2, e, kc * 512:(kc + 1) * 512],
                   start=True, stop=True).then_inc(t_p1, 1)

            def scores(it, lu, kt):
                pe.wait_ge(t_e, at(it, lu, 8, kt + 1))
                if kt == 0:
                    pe.wait_ge(t_miscev, before_unit(it, lu))
                g2 = lu // 4 % 2
                for e in range(2):
                    last = mm(ps_s[kt % 2][:, e * 512:(e + 1) * 512], KT[:, g2, e, kt * P:(kt + 1) * P], QT2[:, lu % 2, :],
                              start=True, stop=True)
                last.then_inc(t_s, 1)

            def weighted(it, lu, kt, start, stop):
                g2 = lu // 4 % 2
                for e in range(2):
                    last = mm(ps_ctx[e * DV:(e + 1) * DV, :], v_nat[:, g2, kt, :], probs[:, kt, e, :], start=start, stop=stop)
                last.then_inc(t_pv, 1)

            pe.wait_ge(t_kpad, 2)
            pe.wait_ge(f_ye, NF)
            for lu, name in PRO[:5]:
                misc(None, lu, name)
            for lu in (-2, -1):
                for name in [n for l, n in PRO if l == lu]:
                    misc(None, lu, name)
                for j in range(16):
                    fill(None, lu, j)
            pe.wait_ge(t_set, 4)
            weighted(None, -1, 0, True, False)
            with pe.Fori(0, UNITS // 8) as it:
                for lu in range(8):
                    for kt in range(8):
                        scores(it, lu, kt)
                        if kt == 0:
                            pe.wait_ge(t_e, at(it, lu, 8, 2))
                            weighted(it, lu - 1, 7, False, True)
                        fill(it, lu, 2 * kt)
                        fill(it, lu, 2 * kt + 1)
                        for name in misc_of(lu, kt):
                            misc(it, lu, name)
                        if kt:
                            pe.wait_ge(t_e, at(it, lu, 8, kt + 2))
                            if kt == 1:
                                pe.wait_ge(t_cev, at(it, lu, 1, 1))
                                pe.wait_ge(t_v[lu // 4 % 2], it * 16 + 16)
                            weighted(it, lu, kt - 1, kt == 1, False)
            pe.wait_ge(t_e, 8 * UNITS + 2)
            weighted(None, UNITS - 1, 7, False, True)
            pe.wait_ge(t_sum, UNITS + 1)
            pe.wait_ge(t_miscev, len(PRO) + 4 * len(BODY))
            for e in range(2):
                last = mm(ps_misc[e * DV:(e + 1) * DV, :], ones[:, 0:DV], acc[:, 1, 0, e, :], start=True, stop=True)
            last.then_inc(t_misc, 1)

            pe.wait_ge(o_w, 16)
            for t in range(NT):
                h = t % 2
                pe.wait_ge(o_ct[t % 4], 16 * (t // 4 + 1))
                if t >= 2:
                    pe.wait_ge(o_done, t - 1)
                for c in range(PAIRS):
                    last = mm(bank[h][:, 0:D], ct[:, t % 4, c, :], wo[:, c, :], start=c == 0, stop=c == PAIRS - 1)
                last.then_inc(o_mm, 1)
    return nc


def make_consts():
    import numpy as np
    c = np.zeros((P, C_ALL), np.float32)
    c[:, C_ID:C_ID + P] = np.eye(P)
    c[:, C_TRI:C_TRI + P] = np.triu(np.ones((P, P)), 1)
    inv = (1.0 / np.float32(10000.0) ** (np.arange(0, DK, 2, dtype=np.float32) / np.float32(DK))).astype(np.float32)
    ang = np.arange(L, dtype=np.float32)[:, None] * inv[None, :]
    sin, cos = np.sin(ang).astype(np.float32), np.cos(ang).astype(np.float32)

    def tiles(a):
        return a.reshape(TB, P, DK).transpose(1, 0, 2).reshape(P, TB * DK)

    c[:, C_COS:C_COS + TB * DK] = tiles(np.concatenate([cos, cos], 1))
    c[:, C_SIN:C_SIN + TB * DK] = tiles(np.concatenate([-sin, sin], 1))
    c[:, C_TIE:C_TIE + E * E] = (np.arange(E)[None, :] < np.arange(E)[:, None]).astype(np.float32).reshape(-1)
    c[:, C_THR:C_THR + NT] = P * np.arange(NT)
    c[:, C_TIX:C_TIX + XTILES] = np.arange(XTILES)
    return c


_INS = ["L0_attn_x", "L0_attn_W_attn", "L0_attn_W_out", "L0_attn_b_out", "L0_ffn_gate_w", "L0_ffn_base_gate_up",
        "L0_ffn_base_down", "L0_ffn_expert_gate_up", "L0_ffn_expert_down"]


def kernel(**inputs):
    import numpy as np
    import concourse.bacc as bacc
    from concourse.bass_utils import run_bass_kernel_spmd

    nc = bacc.Bacc("TRN2", target_bir_lowering=False, num_devices=1)
    arrays, args = {}, []
    for name in _INS:
        a = np.ascontiguousarray(inputs[name])
        arrays[name] = a
        args.append(nc.dram_tensor(name, a.shape, mybir.dt.from_np(a.dtype), kind="ExternalInput").ap())
    arrays["consts"] = make_consts()
    args.append(nc.dram_tensor("consts", arrays["consts"].shape, mybir.dt.float32, kind="ExternalInput").ap())
    args.append(nc.dram_tensor("out", (B, L, D), mybir.dt.float32, kind="ExternalOutput").ap())
    build(nc, *args)
    r = run_bass_kernel_spmd(nc, [arrays], core_ids=[0])
    return r.results[0]["out"]
```

```python
from contextlib import ExitStack

import concourse.bass as bass
import concourse.mybir as mybir

P = 128
B, L, D = 2, 1024, 256
NH, NKV, DK, DV = 16, 4, 16, 64
E, I = 8, 512
TOK = B * L
NT = TOK // P
TB = L // P
KC = D // P
IC = I // P
NHK = NH + NKV
QK_COLS = NHK * DK
VG_COLS = NKV * DV + E
XTILES = 2 * NT + E - 1
NF = NT + XTILES
ROWS = NF * P
RING = 4
LATE = 4
TAIL = 16
ST = 64
MCOL = 48
PAIRS = NH // 2
GROUPS = B * NKV
QH = 512
QT = QH // P
UNITS = GROUPS * 2 * (L // QH)
EPS = 1e-5
SCALE = DK ** -0.5

C_ID, C_TRI, C_COS, C_SIN = 0, 128, 256, 384
C_TIE = 512
C_THR = C_TIE + E * E
C_TIX = C_THR + NT
C_ALL = C_TIX + XTILES


def build(nc, x, w_attn, w_out, b_out, gate_w, base_gu, base_dn, exp_gu, exp_dn, consts, out):
    F32, F32R, I32 = mybir.dt.float32, mybir.dt.float32r, mybir.dt.int32
    ALU, ACT, AX = mybir.AluOpType, mybir.ActivationFunctionType, mybir.AxisListType
    ds = bass.ds
    ctx = ExitStack()
    with ctx:
        def sb(name, shape, dt=F32):
            return ctx.enter_context(nc.sbuf_tensor(name, shape, dt))

        def sb_both(name, shape):
            with nc.sbuf_tensor(name + "_r", shape, F32R) as as_r:
                pass
            return sb(name, shape), as_r

        def sem(name):
            return ctx.enter_context(nc.semaphore(name))

        xd = nc.dram_tensor("xd", (ROWS, D), F32, kind="Internal").ap()
        yd = nc.dram_tensor("yd", (ROWS, D), F32, kind="Internal").ap()
        qd = nc.dram_tensor("qd", ((GROUPS + 1) * 2 * L, P), F32, kind="Internal").ap()
        kd = nc.dram_tensor("kd", ((GROUPS // 2 + 1) * L, 2 * ST), F32, kind="Internal").ap()
        vd = nc.dram_tensor("vd", ((GROUPS // 2 + 1) * L, 2 * DV), F32, kind="Internal").ap()
        cd = nc.dram_tensor("cd", ((UNITS + 2) * P, QH), F32, kind="Internal").ap()

        cst = sb("cst", [P, C_ALL])
        zero = sb("zero", [P, D])
        ones = sb("ones", [P, P])
        bias = sb("bias", [P, D])
        ident = cst[:, C_ID:C_ID + P]
        tri = cst[:, C_TRI:C_TRI + P]
        cosT = cst[:, C_COS:C_COS + TB * DK].rearrange("p (t d) -> p t d", d=DK)
        sinT = cst[:, C_SIN:C_SIN + TB * DK].rearrange("p (t d) -> p t d", d=DK)
        tie = cst[:, C_TIE:C_TIE + E * E].rearrange("p (e f) -> p e f", f=E)
        GU, DN = KC * 2 * I, IC * D
        WS = GU + DN
        big, ring = sb_both("big", [P, RING * 2 * WS + WS])
        probs = big[:, 0:8 * 2 * QH].rearrange("p (k h q) -> p k h q", k=8, h=2)
        acc = big[:, 8192:12288].rearrange("p (u a h q) -> p u a h q", u=2, a=2, h=2)
        ctx_nrm = big[:, 12288:13312].rearrange("p (r q) -> p r q", r=2)
        y_stage = big[:, 13312:15360]
        y_pick_rows = big[:, 15360:15360 + NT * 2 * D]
        y_pick = big[:, 15360:15360 + NT * 2 * D].rearrange("p (t s d) -> p t s d", t=NT, s=2)
        ct = big[:, 23552:27648].rearrange("p (r c q) -> p r c q", r=4, c=8)
        xt4 = big[:, 3 * 2 * WS:3 * 2 * WS + 4 * D].rearrange("p (r d) -> p r d", r=4)
        wo_hi, wo_lo = [ring[:, o:o + 8 * D].rearrange("p (c d) -> p c d", c=8) for o in (8192, 13312)]
        ct_parts = ring[:, 0:8 * 2 * QH].rearrange("p (r i c q) -> p r i c q", r=4, i=2, c=8)
        ct_hi, ct_lo = ct_parts[:, :, 0, :, :], ct_parts[:, :, 1, :, :]
        mid = sb("mid", [P, 4608])
        xs = mid[:, 0:NT * D].rearrange("p (t d) -> p t d", d=D)
        q_nat = mid[:, 0:4 * QT * P].rearrange("p (r t c) -> p r t c", r=4, t=QT)
        k_nat = mid[:, 2048:2048 + TB * 3 * ST].rearrange("p (t c) -> p t c", t=TB)
        v_nat = mid[:, 3584:3584 + 2 * TB * DV].rearrange("p (r t d) -> p r t d", r=2, t=TB)
        KT_raw, KT = sb_both("KT", [P, 2, 2, L])
        QT_raw, QTs = sb_both("QT", [P, 4, QH])
        QT1 = QTs[:, 0:2, :]
        QT2 = QTs[:, 2:4, :]
        base_gu_w = KT[:, :, :, :].rearrange("p a b c -> p (a b c)")
        base_dn_w = QTs[:, :, :].rearrange("p a c -> p (a c)")
        base_gu_raw = KT_raw[:, :, :, :].rearrange("p a b c -> p (a b c)")
        base_dn_raw = QT_raw[:, :, :].rearrange("p a c -> p (a c)")
        w_in, w_in_r = sb_both("w_in", [P, KC, QK_COLS + VG_COLS])
        hidT_lo = w_in_r[:, :, :].rearrange("p k n -> p (k n)")[:, 0:2 * I].rearrange("p (r c) -> p r c", r=2)
        xT_hi = sb("xT_hi", [P, 2, D], F32R)
        xT_lo = sb("xT_lo", [P, 2, D], F32R)
        wrk, wrk_r = sb_both("wrk", [P, 2 * (NHK * ST + NKV * DV + 3 * QK_COLS)])
        stack = wrk[:, 0:2560].rearrange("p (r h c) -> p r h c", r=2, h=NHK)
        v_out = wrk[:, 2560:3072].rearrange("p (r c) -> p r c", r=2)
        rope_a = wrk[:, 3072:3712].rearrange("p (r h c) -> p r h c", r=2, h=NHK)
        rope_b = wrk[:, 3712:4352].rearrange("p (r h c) -> p r h c", r=2, h=NHK)
        roped = wrk[:, 4352:4992].rearrange("p (r h c) -> p r h c", r=2, h=NHK)
        gate_t = wrk[:, 0:1024].rearrange("p (r c) -> p r c", r=2)
        gate_s = wrk[:, 1024:2048].rearrange("p (r c) -> p r c", r=2)
        hid = wrk[:, 2048:3072].rearrange("p (r c) -> p r c", r=2)
        hidT_hi = wrk_r[:, 3072:4096].rearrange("p (r c) -> p r c", r=2)
        y_sb = wrk[:, 4096:4608].rearrange("p (r c) -> p r c", r=2)
        wo = wrk[:, 0:8 * D].rearrange("p (c d) -> p c d", c=8)
        fx = wrk[:, 2048:2048 + 2 * D].rearrange("p (r d) -> p r d", r=2)
        fy = wrk[:, 2560:2560 + 2 * D].rearrange("p (r d) -> p r d", r=2)
        fa = wrk[:, 3072:3072 + 2 * D].rearrange("p (r d) -> p r d", r=2)
        fb = wrk[:, 3584:3584 + 2 * D].rearrange("p (r d) -> p r d", r=2)
        xt_in = sb("xt_in", [P, 2, D])
        xT = sb("xT", [P, 2, D])
        stats = sb("stats", [P, NT, 6])
        mv = sb("mv", [P, NT, 2])
        veps = sb("veps", [P, NT])
        std = sb("std", [P, NT])
        table = sb("table", [P, 1])
        rstd = sb("rstd", [P, NT])
        mpart = sb("mpart", [P, 2, QT * 2 * 2])
        den = xT[:, :, :].rearrange("p r c -> p (r c)")
        lg = sb("lg", [P, NT, E])
        r_gt = sb("r_gt", [P, NT * E * E])
        r_eq = sb("r_eq", [P, NT * E * E])
        rden = r_gt[:, 0:QH]
        ctx_raw = r_eq[:, 0:2 * QH].rearrange("p (r q) -> p r q", r=2)
        rank = sb("rank", [P, NT, E])
        sel = sb("sel", [P, 3, NT, E])
        tmp = sb("tmp", [P, NT, E])
        best = sb("best", [P, 2, NT])
        wts = sb("wts", [P, 4, NT])
        cum = sb("cum", [P, 2, 8 + NT, E])
        cumt = sb("cumt", [P, 2, 4 + E])
        ntl = sb("ntl", [P, E])
        slotf = sb("slotf", [P, NT, E])
        posf = sb("posf", [P, 2, NT])
        pos = sb("pos", [P, 2, NT], I32)
        pos_now = sb("pos_now", [P, 8], I32)
        etf = sb("etf", [P, XTILES])
        nought = sb("nought", [P, 1])
        eslot = sb("eslot", [P, XTILES], I32)
        eready = sb("eready", [P, XTILES], I32)
        efree = sb("efree", [P, E - RING], I32)

        ps_s = [ctx.enter_context(nc.psum_tensor(f"ps_s{i}", [P, 2 * 512], F32)) for i in range(2)]
        ps = [ctx.enter_context(nc.psum_tensor(f"ps{i}", [P, 512], F32)) for i in range(4, 8)]
        bank = [ps_s[0][:, 0:512], ps_s[0][:, 512:1024], ps_s[1][:, 0:512], ps_s[1][:, 512:1024]] + [p[:, :] for p in ps]
        ps_ctx, ps_misc = bank[6], bank[7]

        s_cst, s_win, s_wbase, s_bias = sem("cst_in"), sem("w_in_in"), sem("w_base_in"), sem("bias_in")
        s_wexp = [sem(f"w_expert_in{i}") for i in range(E)]
        w_free, w_hi, w_split, b_hi, b_split = sem("w_place_free"), sem("w_high_parts"), sem("w_expert_split"), sem("w_base_high"), sem("w_base_split")
        r_tab, f_xtl, f_htl = sem("r_tables_ready"), sem("f_xT_low_ready"), sem("f_hT_low_ready")
        s_x = [sem(f"x_in{i}") for i in range(4)]
        s_mem = sem("constants_set")
        s_zero, s_tail = sem("slots_zeroed"), sem("tails_zeroed")
        s_bn, s_mv, s_veps, s_std, s_rstd = sem("bn_done"), sem("mv_done"), sem("veps_done"), sem("std_done"), sem("rstd_done")
        a_xn = sem("a_xn_ready")
        a_xl = sem("a_xn_tile")
        a_xtp, a_xt = sem("a_xT_in_psum"), sem("a_xT_ready")
        a_qk, a_vg = sem("a_qk_in_psum"), sem("a_vg_in_psum")
        a_vev = sem("a_v_evacuated")
        a_ra, a_rb = sem("a_rope_cos"), sem("a_rope_sin")
        a_ro, a_hi, a_lo = sem("a_roped"), sem("a_high_part"), sem("a_low_part")
        a_qst = [sem(f"a_qkv_stored{i}") for i in range(2)]
        r_ch, r_sel, r_cnt, r_d, r_e, r_pos = sem("r_chain"), sem("r_selected"), sem("r_counted"), sem("r_diff"), sem("r_exp"), sem("r_pos_ready")
        s_disp = sem("rows_dispatched")
        f_xl = [sem(f"f_x_loaded{i}") for i in range(2)]
        f_xtp, f_xt = sem("f_xT_in_psum"), sem("f_xT_ready")
        f_g, f_u, f_th, f_s, f_h = sem("f_gate_in_psum"), sem("f_up_in_psum"), sem("f_tanh"), sem("f_gate_silu"), sem("f_hidden")
        f_htp, f_ht, f_y, f_ye = sem("f_hT_in_psum"), sem("f_hT_ready"), sem("f_y_in_psum"), sem("f_y_evacuated")
        f_ys = [sem(f"f_y_stored{i}") for i in range(2)]
        t_q = [sem(f"t_q_loaded{i}") for i in range(4)]
        t_k, t_v = sem("t_k_loaded"), [sem(f"t_v_loaded{i}") for i in range(2)]
        t_kpad = sem("t_k_padding")
        t_misc, t_miscev = sem("t_misc_in_psum"), sem("t_misc_evacuated")
        t_p1, t_red, t_negm = sem("t_pass1_in_psum"), sem("t_pass1_reduced"), sem("t_negmax_ready")
        t_s, t_e, t_pv = sem("t_scores_in_psum"), sem("t_exp_done"), sem("t_pv_done")
        t_add, t_sum, t_cev = sem("t_probs_added"), sem("t_probs_summed"), sem("t_ctx_evacuated")
        t_rd, t_nrm = sem("t_den_inverted"), sem("t_ctx_normalised")
        t_cst = [sem(f"t_ctx_stored{i}") for i in range(2)]
        t_set = sem("t_standin_set")
        o_pick = sem("o_rows_in_place")
        o_now = sem("o_slots_copied")
        o_whi, o_wlo, o_hi, o_lo = sem("o_w_high"), sem("o_w_low"), sem("o_ctx_high"), sem("o_ctx_low")
        o_w = sem("o_w_in")
        o_in = [sem(f"o_tile_in{i}") for i in range(2)]
        o_ct = [sem(f"o_ctx_in{i}") for i in range(4)]
        o_y = [sem(f"o_rows_picked{i}") for i in range(4)]
        o_mm, o_f, o_done = sem("o_in_psum"), sem("o_chain"), sem("o_ready")
        o_st = [sem(f"o_stored{i}") for i in range(2)]

        PRO = [(-3, "T1"), (-3, "K0"), (-3, "K1"), (-3, "K2"), (-3, "K3"), (-2, "T1"), (-1, "T1"), (-1, "T2")]
        SLOT = {"T1": 0, "K0": 1, "K2": 1, "T2": 3, "DEN": 5, "K1": 6, "K3": 6}
        BODY = []
        for lu in range(8):
            k = {0: ["K0", "K1"], 1: ["K2", "K3"]}.get(lu % 4, [])
            BODY += [(lu, n) for n in sorted(["T1", "T2", "DEN"] + k, key=lambda n: SLOT[n])]

        def misc_index(it, lu, name):
            if it is None:
                return PRO.index((lu, name)) if lu < 0 else len(PRO) + 4 * len(BODY)
            return it * len(BODY) + (len(PRO) + BODY.index((lu, name)))

        def before_unit(it, lu):
            if it is None:
                return {-2: 5, -1: 6}[lu]
            if lu == 0:
                return it * len(BODY) + len(PRO)
            return misc_index(it, lu - 1, "K3" if lu % 4 == 2 else "T2") + 1

        def misc_before(it, lu, m):
            return it * len(BODY) + (len(PRO) + len([n for l, n in BODY if l < lu or (l == lu and SLOT[n] <= 2 * m)]))

        FILL_BANK = [4, 5, 7, 4, 5, 4, 7, 5]
        FILL_AGO = [3, 2, 4, 3, 3, 2, 4, 3]

        def misc_of(lu, slot):
            return [n for l, n in BODY if l == lu and SLOT[n] == slot]

        def at(it, lu, per, plus=0):
            return per * lu + plus if it is None else it * (8 * per) + (per * lu + plus)

        YS_ALL = [16 + 16 * ((NF + 1 - h) // 2) for h in range(2)]

        def base_part(q):
            third = slice(q * DN, (q + 1) * DN) if q < 2 else slice(0, DN)
            low = slice(third.start + (GU if q < 2 else DN), third.stop + (GU if q < 2 else DN))
            raw, w = (base_gu_raw, base_gu_w) if q < 2 else (base_dn_raw, base_dn_w)
            return raw[:, low], w[:, third], w[:, low]

        fills = [[(lu, j) for j in range(16)] for lu in (-2, -1)]
        items = PRO[:6] + fills[0] + PRO[6:] + fills[1]
        gaps = {}
        g = 0
        for k, item in enumerate(items):
            gaps[divmod(3 * (NF - TAIL) + g, 3)] = (item, items[k - 1] if k else None)
            g += 1

        block = ctx.enter_context(nc.Block())

        @block.sync
        def _(sp):
            xv = x.rearrange("b (t p) d -> p (b t) d", p=P)
            for j in range(4):
                sp.dma_start(xs[:, 4 * j:4 * j + 4, :], xv[:, 4 * j:4 * j + 4, :]).then_inc(s_x[j], 16)
                if j == 0:
                    sp.dma_start(cst[:, :], consts).then_inc(s_cst, 16)
                if j == 1:
                    sp.dma_start(w_in[:, :, 0:QK_COLS + NKV * DV], w_attn.rearrange("(k p) n -> p k n", p=P)).then_inc(s_win, 16)
                    sp.dma_start(w_in[:, :, QK_COLS + NKV * DV:], gate_w.rearrange("(k p) n -> p k n", p=P)).then_inc(s_win, 16)
            sp.dma_start(bias[:, :], b_out.partition_broadcast(P)).then_inc(s_bias, 16)
            for b in range(B):
                qb = qd[b * PAIRS * L:(b + 1) * PAIRS * L, :].rearrange("(c t) e -> t c e", c=PAIRS)
                kb = kd[b * NKV // 2 * L:(b + 1) * NKV // 2 * L, :].rearrange("(c t) e -> t c e", c=NKV // 2)
                vb = vd[b * NKV // 2 * L:(b + 1) * NKV // 2 * L, :].rearrange("(c t) e -> t c e", c=NKV // 2)
                with sp.Fori(0, TB // 2) as i:
                    for h in range(2):
                        t = i * 2 + (b * TB + h)
                        row = i * (2 * P) + h * P
                        sp.wait_ge(a_vev, t + 1)
                        sp.dma_start(vb[ds(row, P), :, :], v_out[:, h, :].rearrange("p (c d) -> p c d", c=NKV // 2)).then_inc(a_qst[h], 16)
                        sp.wait_ge(a_lo, 2 * t + 1)
                        sp.dma_start(qb[ds(row, P), :, :], stack[:, h, 0:NH, :].rearrange("p (c e) k -> p c (e k)", c=PAIRS)).then_inc(a_qst[h], 16)
                        sp.wait_ge(a_lo, 2 * t + 2)
                        sp.dma_start(kb[ds(row, P), :, :], stack[:, h, NH:NHK, :].rearrange("p (c e) k -> p c (e k)", e=2)).then_inc(a_qst[h], 16)

            def load_base(n, h):
                sp.wait_ge(f_xtp, n - 1)
                sp.dma_start(xt_in[:, h:h + 1, :], xs[:, ds(n, 1), :]).then_inc(f_xl[h], 16)

            def load_x(n, h):
                sp.wait_ge(f_xtp, n - 1)
                k = n - NT
                split_by = sp.value_load(eready[0:1, k:k + 1] if isinstance(k, int) else eready[0:1, ds(k, 1)],
                                         min_val=1, max_val=E)
                sp.wait_ge(w_split, split_by)
                sp.dma_start(xt_in[:, h, :], xd[ds(n * P, P), :]).then_inc(f_xl[h], 16)

            def store_y(n, h):
                sp.wait_ge(f_ye, n + 1)
                sp.dma_start(yd[ds(n * P, P), :], y_sb[:, h, :]).then_inc(f_ys[h], 16)

            load_base(2, 0)
            with sp.Fori(0, (NT - 4) // 2) as i:
                for h in range(2):
                    n = i * 2 + (1 + h)
                    load_base(n + 2, (1 + h) % 2)
                    store_y(n - 1, h)
            load_base(NT - 1, 1)
            store_y(NT - 4, 0)
            sp.dma_start(qd[GROUPS * 2 * L:, :].rearrange("(k p) d -> p k d", p=P),
                          zero[:, 0:P].unsqueeze(1).to_broadcast([P, 2 * L // P, P])).then_inc(s_tail, 16)
            sp.dma_start(kd[GROUPS // 2 * L:, :].rearrange("(k p) d -> p k d", p=P),
                          zero[:, 0:2 * ST].unsqueeze(1).to_broadcast([P, L // P, 2 * ST])).then_inc(s_tail, 16)
            sp.dma_start(vd[GROUPS // 2 * L:, :].rearrange("(k p) d -> p k d", p=P),
                          zero[:, 0:2 * DV].unsqueeze(1).to_broadcast([P, L // P, 2 * DV])).then_inc(s_tail, 16)
            sp.wait_ge(s_disp, 16 * 2 * NT)
            sp.wait_ge(r_tab, 3)
            def move_xy(steps, n0):
                with sp.Fori(0, steps // 2) as i:
                    for h in range(2):
                        n = i * 2 + (n0 + h)
                        load_x(n + 2, (n0 + h) % 2)
                        store_y(n - 1, (n0 + h + 1) % 2)

            move_xy(20, NT - 2)

            def load_q(v, r):
                sp.dma_start(q_nat[:, r, :, :], qd[ds(v * QH, QH), :].rearrange("(t p) c -> p t c", p=P)).then_inc(t_q[r], 16)

            def load_k(it, g):
                sp.dma_start(k_nat[:, :, ST:2 * ST],
                             kd[ds(it * L + g // 2 * L, L), g % 2 * ST:(g % 2 + 1) * ST].rearrange("(t p) c -> p t c", p=P)).then_inc(t_k, 16)

            def load_v(it, g):
                sp.dma_start(v_nat[:, g % 2, :, :],
                             vd[ds(it * L + g // 2 * L, L), g % 2 * DV:(g % 2 + 1) * DV].rearrange("(t p) c -> p t c", p=P)).then_inc(t_v[g % 2], 16)

            for h in range(2):
                sp.wait_ge(a_qst[h], 16 + 48 * (NT // 2))
            sp.wait_ge(s_tail, 16 * 3)
            sp.wait_ge(f_xtp, NT)
            for v in range(4):
                load_q(v, v)
            load_k(0, 0)
            load_v(0, 0)
            move_xy(NF - 2 - (NT + 18) - 1, NT + 18)
            load_x(NF - 1, (NF - 1) % 2)
            sp.wait_ge(t_misc, 5)
            load_k(0, 1)
            for n in (NF - 4, NF - 3, NF - 2, NF - 1):
                store_y(n, n % 2)
            for h in range(2):
                sp.wait_ge(f_ys[h], YS_ALL[h])
            sp.dma_start(wo, w_out.rearrange("(c p) d -> p c d", p=P)).then_inc(o_w, 16)
            with sp.Fori(0, UNITS // 8) as it:
                for lu in range(8):
                    sp.wait_ge(t_misc, before_unit(it, lu))
                    load_q(at(it, lu, 1, 4), lu % 4)
                    if lu % 4 == 0:
                        sp.wait_ge(t_pv, at(it, lu, 8, 8))
                        load_v(it, lu // 4 + 1)
                    if lu % 4 == 2:
                        sp.wait_ge(t_misc, misc_index(it, lu - 1, "K3") + 1)
                        load_k(it, lu // 4 + 2)
                    sp.wait_ge(t_nrm, at(it, lu, 1, 3))
                    sp.dma_start(cd[ds(at(it, lu, 1) * P, P), :], ctx_nrm[:, lu % 2, :]).then_inc(t_cst[lu % 2], 16)
                for j in range(4):
                    sp.wait_ge(o_y[j], it * 32 + 32)
                sp.dma_start(y_pick_rows[:, ds(it * (8 * D), 8 * D)], y_stage).then_inc(o_pick, 16)
            xo = x.rearrange("b (t p) d -> (b t) p d", p=P)
            def load_ctx(t):
                b, tb = divmod(t, TB)
                half, q0 = divmod(tb, QT)
                if t == 0:
                    for h in range(2):
                        sp.wait_ge(t_cst[h], 16 + 16 * (UNITS // 4 + 1))
                if t == TB:
                    for h in range(2):
                        sp.wait_ge(t_nrm, UNITS + 3 + h)
                        sp.dma_start(cd[(UNITS + h) * P:(UNITS + h + 1) * P, :], ctx_nrm[:, h, :]).then_inc(t_cst[h], 16)
                    for h in range(2):
                        sp.wait_ge(t_cst[h], 16 + 16 * (UNITS // 2 + 1))
                if t >= 4:
                    sp.wait_ge(o_lo, t - 3)
                src = cd[P * (2 + b * 16):P * (2 + (b + 1) * 16), :].rearrange("(c s p) q -> s p c q", s=2, p=P)
                sp.dma_start(ct[:, t % 4, :, :], src[half, :, :, q0 * P:(q0 + 1) * P]).then_inc(o_ct[t % 4], 16)

            def load_rows(t):
                if t >= 2:
                    sp.wait_ge(o_done, t - 1)
                sp.dma_start(fx[:, t % 2, :], xo[t]).then_inc(o_in[t % 2], 16)
                sp.dma_start(fy[:, t % 2, :], yd[t * P:(t + 1) * P, :]).then_inc(o_in[t % 2], 16)

            for t in range(NT + 2):
                if t < NT:
                    load_ctx(t)
                if t >= 2:
                    load_rows(t - 2)

        @block.gpsimd
        def _(pool):
            nc.gpsimd.memset(zero[:, :], 0.0).then_inc(s_mem, 1)
            nc.gpsimd.memset(ones[:, :], 1.0).then_inc(s_mem, 1)
            nc.gpsimd.memset(stack[:, :, :, MCOL:], 0.0).then_inc(s_mem, 1)
            pool.wait_ge(s_mem, 3)
            nc.gpsimd.memset(stack[:, :, NH:, MCOL:MCOL + 1], 1.0).then_inc(s_mem, 1)
            nc.gpsimd.memset(cum[:, :, :, :], 0.0).then_inc(s_mem, 1)
            nc.gpsimd.memset(cumt[:, :, :], 0.0).then_inc(s_mem, 1)
            nc.gpsimd.memset(nought[:, :], 0.0).then_inc(s_mem, 1)
            pool.wait_ge(s_mem, 7)
            pool.wait_ge(a_xn, 4)
            for t in range(4):
                nc.gpsimd.tensor_scalar(xt4[:, t, :], xs[:, t, :], 1.0, 0.0, ALU.mult, ALU.add).then_inc(a_xl, 1)

            def low_parts(t, h):
                pool.wait_ge(a_hi, 2 * t + 2)
                nc.gpsimd.tensor_tensor(stack[:, h, 0:NH, 2 * DK:3 * DK].bitcast(F32R), roped[:, h, 0:NH, :],
                                        stack[:, h, 0:NH, 0:DK], ALU.subtract).then_inc(a_lo, 1)
                nc.gpsimd.tensor_tensor(stack[:, h, NH:, DK:2 * DK].bitcast(F32R), roped[:, h, NH:, :],
                                        stack[:, h, NH:, 0:DK], ALU.subtract).then_inc(a_lo, 1)

            with pool.Fori(0, NT // 4 - 1) as i:
                for j in range(4):
                    t = i * 4 + j
                    low_parts(t, j % 2)
                    pool.wait_ge(a_xtp, t + 1)
                    pool.wait_ge(a_xn, t + 5)
                    nc.gpsimd.tensor_tensor(xt4[:, j:j + 1, :], xs[:, ds(t + 4, 1), :], zero[:, :].unsqueeze(1), ALU.add).then_inc(a_xl, 1)
            for t in range(NT - 4, NT):
                low_parts(t, t % 2)
                if t < NT - 2:
                    h = t % 2
                    nc.gpsimd.tensor_scalar(xt_in[:, h, :], xs[:, h, :], 1.0, 0.0, ALU.mult, ALU.add).then_inc(a_xl, 1)
            pool.wait_ge(a_xtp, NT)

            def split(e):
                o = e % RING * 2 * WS
                hi, lo, raw = ring[:, o:o + WS], ring[:, o + WS:o + 2 * WS], big[:, o + WS:o + 2 * WS]
                pool.wait_ge(s_wexp[e], 32)
                nc.gpsimd.tensor_scalar(hi, raw, 1.0, 0.0, ALU.mult, ALU.add).then_inc(w_hi, 1)
                pool.wait_ge(w_hi, e + 1)
                nc.gpsimd.tensor_tensor(lo, raw, hi.bitcast(F32), ALU.subtract).then_inc(w_split, 1)

            for e in range(RING - 1):
                split(e)
            pool.wait_ge(s_zero, 16 * 4)
            pool.wait_ge(r_pos, 2)
            for t in range(NT):
                for s in range(2):
                    pool.indirect_dma_start(xd, bass.IndirectOffsetOnAxis(ap=pos[:, s, t:t + 1], axis=0),
                                            xs[:, t, :], None).then_inc(s_disp, 16)
            split(RING - 1)
            pool.wait_ge(r_tab, 3)
            pool.wait_ge(s_disp, 16 * 2 * NT)
            pool.wait_ge(f_xtp, NT)
            nc.gpsimd.memset(k_nat[:, :, 0:ST], 0.0).then_inc(t_kpad, 1)
            nc.gpsimd.memset(k_nat[:, :, 2 * ST:], 0.0).then_inc(t_kpad, 1)
            nc.gpsimd.memset(v_nat[:, 1, :, :], 0.0).then_inc(t_set, 1)
            nc.gpsimd.memset(den, 1.0).then_inc(t_set, 1)
            nc.gpsimd.memset(rden, 1.0).then_inc(t_set, 1)
            nc.gpsimd.memset(ctx_raw[:, 0, :], 1.0).then_inc(t_set, 1)
            for e in range(RING, E):
                tiles = pool.value_load(efree[0:1, e - RING:e - RING + 1], min_val=NT, max_val=NF)
                pool.wait_ge(f_y, tiles)
                nc.gpsimd.tensor_tensor(nought[:, :], nought[:, :], nought[:, :], ALU.add).then_inc(w_free, 1)
                pool.wait_ge(w_free, e - RING + 1)
                o = e % RING * 2 * WS + WS
                pool.dma_start(big[:, o:o + GU].rearrange("p (k n) -> p k n", k=KC),
                               exp_gu[e].rearrange("(k p) n -> p k n", p=P)).then_inc(s_wexp[e], 16)
                pool.dma_start(big[:, o + GU:o + WS].rearrange("p (k n) -> p k n", k=IC),
                               exp_dn[e].rearrange("(k p) n -> p k n", p=P)).then_inc(s_wexp[e], 16)
                split(e)
            pool.wait_ge(f_y, NF - 2)
            nc.gpsimd.memset(probs[:, 6:8, :, :], 1.0).then_inc(t_set, 1)
            nc.gpsimd.memset(acc[:, 1, :, :, :], 1.0).then_inc(t_set, 1)
            pool.sem_inc(t_add, 6)
            for h in range(2):
                pool.wait_ge(f_ys[h], YS_ALL[h])
            with pool.Fori(0, UNITS // 8) as it:
                for lu in range(8):
                    u2 = lu % 2
                    if lu == 0:
                        pool.wait_ge(o_pick, it * 16 + 16)
                    nc.gpsimd.tensor_copy(pos_now[:, lu:lu + 1], pos[:, lu % 2, ds(it * 4 + lu // 2, 1)]).then_inc(o_now, 1)
                    for a, (first, kt) in enumerate([(0, 1), (2, 3), (None, 4), (None, 5), (None, 6), (None, 7)]):
                        pool.wait_ge(t_e, at(it, lu, 8, kt + 3))
                        o = acc[:, u2, a % 2, :, :]
                        if first is None:
                            pool.wait_ge(t_add, at(it, lu, 6, 6 + a - 1))
                            nc.gpsimd.tensor_tensor(o, o, probs[:, kt, :, :], ALU.add).then_inc(t_add, 1)
                        else:
                            if a == 0:
                                if lu:
                                    pool.wait_ge(t_misc, misc_index(it, lu - 1, "DEN") + 1)
                                else:
                                    pool.wait_ge(t_misc, it * len(BODY) + len(PRO))
                            if a == 1:
                                pool.wait_ge(o_now, at(it, lu, 1, 1))
                            nc.gpsimd.tensor_tensor(o, probs[:, first, :, :], probs[:, kt, :, :], ALU.add).then_inc(t_add, 1)
                            if a == 1:
                                pool.indirect_dma_start(y_stage[:, lu * D:(lu + 1) * D], None, yd,
                                                        bass.IndirectOffsetOnAxis(ap=pos_now[:, lu:lu + 1], axis=0)).then_inc(o_y[lu // 2], 16)
            for t in range(NT):
                pool.wait_ge(o_hi, t + 1)
                nc.gpsimd.tensor_tensor(ct_lo[:, t % 4, :, :], ct[:, t % 4, :, :], ct_hi[:, t % 4, :, :].bitcast(F32),
                                        ALU.subtract).then_inc(o_lo, 1)

        @block.scalar
        def _(act):
            def load_expert(e):
                o = e * 2 * WS + WS
                act.dma_start(big[:, o:o + GU].rearrange("p (k n) -> p k n", k=KC),
                              exp_gu[e].rearrange("(k p) n -> p k n", p=P)).then_inc(s_wexp[e], 16)
                act.dma_start(big[:, o + GU:o + WS].rearrange("p (k n) -> p k n", k=IC),
                              exp_dn[e].rearrange("(k p) n -> p k n", p=P)).then_inc(s_wexp[e], 16)

            for h in range(2):
                act.sem_inc(a_qst[h], 16)
                act.sem_inc(f_ys[h], 16)
                act.sem_inc(t_cst[h], 16)
                act.sem_inc(o_st[h], 16)
            act.sem_inc(o_pick, 16)
            act.sem_inc(t_e, 2)
            act.sem_inc(t_pv, 5)
            act.sem_inc(t_nrm, 2)
            def std_of(first, n):
                act.wait_ge(s_veps, first + n)
                nc.scalar.activation(std[:, first:first + n], veps[:, first:first + n], ACT.Sqrt).then_inc(s_std, n)

            std_of(0, 4)
            std_of(4, 2)
            std_of(6, 2)
            act.dma_start(base_gu_raw[:, GU:].rearrange("p (k n) -> p k n", k=KC),
                          base_gu.rearrange("(k p) n -> p k n", p=P)).then_inc(s_wbase, 16)
            act.dma_start(base_dn_raw[:, DN:].rearrange("p (k n) -> p k n", k=IC),
                          base_dn.rearrange("(k p) n -> p k n", p=P)).then_inc(s_wbase, 16)
            act.sem_inc(a_vg, 2)
            act.sem_inc(a_ro, 2)

            def a_xT_out(t, h):
                act.wait_ge(a_xtp, t + 1)
                act.wait_ge(a_vg, t + 1)
                nc.scalar.activation(xT[:, h, :], bank[5 * h][:, 0:D], ACT.Copy).then_inc(a_xt, 1)

            def a_out(t, h, stored):
                act.wait_ge(a_vg, t + 3)
                act.wait_ge(a_qst[h], stored)
                act.wait_ge(a_ro, t + 3)
                nc.scalar.activation(stack[:, h, 0:NH, 0:2 * DK].rearrange("p h (c k) -> p h c k", c=2).bitcast(F32R),
                                     roped[:, h, 0:NH, :].unsqueeze(2).to_broadcast([P, NH, 2, DK]), ACT.Copy).then_inc(a_hi, 1)
                nc.scalar.activation(stack[:, h, NH:, 0:4 * DK].rearrange("p h (c k) -> p h c k", c=2)[:, :, :, 0:DK].bitcast(F32R),
                                     roped[:, h, NH:, :].unsqueeze(2).to_broadcast([P, NKV, 2, DK]), ACT.Copy).then_inc(a_hi, 1)
                nc.scalar.activation(v_out[:, h, :], bank[3 + h][:, 0:NKV * DV], ACT.Copy)
                nc.scalar.activation(lg[:, ds(t, 1), :], bank[3 + h][:, NKV * DV:VG_COLS].unsqueeze(1), ACT.Copy).then_inc(a_vev, 1)

            a_xT_out(0, 0)
            for q in range(4):
                for h in range(2):
                    t = 2 * q + h
                    a_xT_out(t + 1, 1 - h)
                    a_out(t, h, 16 + 48 * q)
                    if h == 0:
                        std_of(8 + 2 * q, 2)
                if q < 3:
                    raw, hi, _ = base_part(q)
                    act.wait_ge(s_wbase, 32)
                    nc.scalar.activation(hi, raw, ACT.Copy).then_inc(b_hi, 1)
            with act.Fori(0, NT // 2 - 5) as i:
                for h in range(2):
                    t = i * 2 + (8 + h)
                    a_xT_out(t + 1, 1 - h)
                    a_out(t, h, i * 48 + (16 + 48 * 4))
            a_xT_out(NT - 1, 1)
            a_out(NT - 2, 0, 16 + 48 * (NT // 2 - 1))
            a_out(NT - 1, 1, 16 + 48 * (NT // 2 - 1))
            def ev_xT(n, h):
                act.wait_ge(f_xtp, n + 1)
                nc.scalar.activation(xT_hi[:, h, :], bank[0][:, 0:D], ACT.Copy).then_inc(f_xt, 1)

            def tanh(n, h):
                act.wait_ge(f_g, n + 1)
                nc.scalar.activation(gate_t[:, h, :], bank[1 + 2 * h], ACT.Tanh, scale=0.5).then_inc(f_th, 1)

            def ev_hT(n, h):
                act.wait_ge(f_htp, n + 1)
                nc.scalar.activation(hidT_hi[:, h, :], bank[5], ACT.Copy).then_inc(f_ht, 1)

            ev_xT(0, 0)
            nc.scalar.activation(table[:, :], zero[:, 0:1], ACT.Tanh)
            for h in range(2):
                act.wait_ge(a_qst[h], 16 + 48 * (NT // 2))
            load_expert(0)
            tanh(0, 0)
            ev_xT(1, 1)
            load_expert(1)

            def act_step(n, h):
                tanh(n, h)
                ev_hT(n - 1, 1 - h)
                act.wait_ge(f_u, n)
                ev_xT(n + 1, 1 - h)

            for n in range(1, 5):
                act_step(n, n % 2)
                k0, k1 = XTILES * (n - 1) // 4, XTILES * n // 4
                act.dma_start(xd[TOK + k0 * P:TOK + k1 * P, :].rearrange("(k p) d -> p k d", p=P),
                              zero[:, :].unsqueeze(1).to_broadcast([P, k1 - k0, D])).then_inc(s_zero, 16)
                if n % 2 == 0:
                    load_expert(n // 2 + 1)
            n0 = 5
            with act.Fori(0, (NF - TAIL - n0) // 2) as i:
                for h in range(2):
                    act_step(i * 2 + (n0 + h), 1 - h)

            def ev_misc(it, lu, name):
                act.wait_ge(t_misc, misc_index(it, lu, name) + 1)
                if name == "T1":
                    dst = QT1[:, (lu + 3) % 2, :]
                elif name == "T2":
                    dst = QT2[:, (lu + 1) % 2, :]
                elif name == "DEN":
                    act.wait_ge(t_rd, at(it, lu, 4, 2))
                    dst = den
                else:
                    g2 = 0 if lu < 0 else (lu // 4 + 1) % 2
                    k = int(name[1])
                    dst = KT[:, g2, k // 2, (k % 2) * 512:(k % 2 + 1) * 512]
                nc.scalar.activation(dst, ps_misc, ACT.Copy).then_inc(t_miscev, 1)

            ADDS = [1, 1, 2, 2, 3, 4, 5, 6]
            def act_gap(n, gap):
                item, _ = gaps.get((n, gap), ((0, 0), None))
                if isinstance(item[1], str):
                    ev_misc(None, *item)

            for n in range(NF - TAIL, NF):
                tanh(n, n % 2)
                act_gap(n, 0)
                ev_hT(n - 1, 1 - n % 2)
                act_gap(n, 1)
                if n + 1 < NF:
                    act.wait_ge(f_u, n)
                    ev_xT(n + 1, 1 - n % 2)
                act_gap(n, 2)
            ev_hT(NF - 1, (NF - 1) % 2)
            act.wait_ge(r_d, 1)
            nc.scalar.activation(wts[:, 1, :], wts[:, 0, :], ACT.Exp).then_inc(r_e, 1)
            with act.Fori(0, UNITS // 8) as it:
                for lu in range(8):
                    for m in range(4):
                        for name in misc_of(lu, 2 * m):
                            ev_misc(it, lu, name)
                        for kt in (2 * m, 2 * m + 1):
                            act.wait_ge(t_s, at(it, lu, 8, kt + 1))
                            act.wait_ge(t_pv, at(it, lu, 8, kt + 1))
                            act.wait_ge(t_add, at(it, lu, 6, ADDS[kt]))
                            nc.scalar.activation(probs[:, kt, :, :], ps_s[kt % 2][:, :].rearrange("p (h q) -> p h q", h=2),
                                                 ACT.Exp, scale=SCALE).then_inc(t_e, 1)
                        if m == 0:
                            act.wait_ge(t_pv, at(it, lu, 8, 8))
                            act.wait_ge(t_nrm, at(it, lu, 1, 2))
                            nc.scalar.activation(ctx_raw[:, (lu + 1) % 2, :], ps_ctx, ACT.Copy).then_inc(t_cev, 1)
                        for name in misc_of(lu, 2 * m + 1):
                            ev_misc(it, lu, name)


            def ctx_high(t):
                act.wait_ge(o_ct[t % 4], 16 * (t // 4 + 1))
                if t >= 4:
                    act.wait_ge(o_mm, t - 3)
                else:
                    act.wait_ge(t_pv, 8 * UNITS + 2 * t + 2)
                    act.wait_ge(t_add, 6 * UNITS + (1, 2, 4, 6)[t])
                nc.scalar.activation(ct_hi[:, t % 4, :, :], ct[:, t % 4, :, :], ACT.Copy).then_inc(o_hi, 1)

            ctx_high(0)
            ctx_high(1)
            act.wait_ge(t_pv, 8 * UNITS + 8)
            act.wait_ge(t_nrm, UNITS + 2)
            nc.scalar.activation(ctx_raw[:, 1, :], ps_ctx, ACT.Copy).then_inc(t_cev, 1)
            ctx_high(2)
            ov = out.rearrange("b (t p) d -> (b t) p d", p=P)
            for t in range(NT):
                if t + 3 < NT:
                    ctx_high(t + 3)
                if t == LATE - 1:
                    act.wait_ge(t_misc, len(PRO) + 4 * len(BODY) + 1)
                    act.wait_ge(t_rd, 4 * UNITS + 2)
                    nc.scalar.activation(den, ps_misc, ACT.Copy).then_inc(t_miscev, 1)
                act.wait_ge(o_done, t + 1)
                act.dma_start(ov[t], fb[:, t % 2, :]).then_inc(o_st[t % 2], 16)
            for h in range(2):
                act.wait_ge(o_st[h], 16 + 16 * (NT // 2))

        @block.vector
        def _(dve):
            def layer_norm(tiles):
                dve.wait_ge(s_x[tiles[0] // 4], 16)
                for t in tiles:
                    nc.vector.bn_stats(stats[:, t, :], xs[:, t, :]).then_inc(s_bn, 1)
                for t in tiles:
                    dve.wait_ge(s_bn, t + 1)
                    nc.vector.bn_aggr(mv[:, t, :], stats[:, t, :]).then_inc(s_mv, 1)
                some = slice(tiles[0], tiles[-1] + 1)
                dve.wait_ge(s_mv, tiles[-1] + 1)
                nc.vector.tensor_scalar(veps[:, some], mv[:, some, 1], EPS, None, ALU.add).then_inc(s_veps, len(tiles))
                dve.wait_ge(s_std, tiles[-1] + 1)
                nc.vector.reciprocal(rstd[:, some], std[:, some]).then_inc(s_rstd, len(tiles))
                dve.wait_ge(s_rstd, tiles[-1] + 1)
                for t in tiles:
                    nc.vector.tensor_scalar(xs[:, t, :], xs[:, t, :], mv[:, t, 0:1], rstd[:, t:t + 1],
                                            ALU.subtract, ALU.mult).then_inc(a_xn, 1)

            def rope(t):
                h = t % 2
                dve.wait_ge(a_qk, t + 1)
                qk = bank[1 + h][:, 0:QK_COLS].rearrange("p (h c) -> p h c", c=DK)
                H2 = DK // 2
                cs = cosT[:, t % TB, :].unsqueeze(1).to_broadcast([P, NHK, DK])
                sn = sinT[:, t % TB, :].unsqueeze(1).to_broadcast([P, NHK, DK])
                nc.vector.tensor_tensor(rope_a[:, h, :, :], qk, cs, ALU.mult).then_inc(a_ra, 1)
                nc.vector.tensor_tensor(rope_b[:, h, :, 0:H2], qk[:, :, H2:], sn[:, :, 0:H2], ALU.mult).then_inc(a_rb, 1)
                nc.vector.tensor_tensor(rope_b[:, h, :, H2:], qk[:, :, 0:H2], sn[:, :, H2:], ALU.mult).then_inc(a_rb, 1)
                dve.wait_ge(a_ra, t + 1)
                dve.wait_ge(a_rb, 2 * t + 2)
                if t >= 2:
                    dve.wait_ge(a_lo, 2 * t - 2)
                nc.vector.tensor_tensor(roped[:, h, :, :], rope_a[:, h, :, :], rope_b[:, h, :, :], ALU.add).then_inc(a_ro, 1)

            layer_norm([0, 1, 2, 3])
            layer_norm([4, 5])
            layer_norm([6, 7])
            dve.wait_ge(s_cst, 16)
            for t in range(NT):
                rope(t)
                if t % 2 == 0 and t + 9 < NT:
                    layer_norm([t + 8, t + 9])
                if t in (3, 5, 7):
                    q = (t - 3) // 2
                    raw, hi, lo = base_part(q)
                    dve.wait_ge(b_hi, q + 1)
                    nc.vector.tensor_tensor(lo, raw, hi.bitcast(F32), ALU.subtract).then_inc(b_split, 1)

            def gate_silu(n, h):
                dve.wait_ge(f_th, n + 1)
                V.scalar_tensor_tensor(gate_s[:, h, :], gate_t[:, h, :], 1.0, bank[1 + 2 * h], ALU.add, ALU.mult).then_inc(f_s, 1)

            def gate_up(n, h):
                dve.wait_ge(f_s, n + 1)
                dve.wait_ge(f_u, n + 1)
                V.scalar_tensor_tensor(hid[:, h, :], gate_s[:, h, :], 0.5, bank[2 + 2 * h], ALU.mult, ALU.mult).then_inc(f_h, 1)

            def low_xT(n, h):
                dve.wait_ge(f_xt, n + 1)
                V.tensor_tensor(xT_lo[:, h, :], bank[0][:, 0:D], xT_hi[:, h, :].bitcast(F32), ALU.subtract).then_inc(f_xtl, 1)

            def low_hT(n, h):
                dve.wait_ge(f_ht, n + 1)
                V.tensor_tensor(hidT_lo[:, h, :], bank[5], hidT_hi[:, h, :].bitcast(F32), ALU.subtract).then_inc(f_htl, 1)

            def ev_y(n, h):
                dve.wait_ge(f_y, n + 1)
                V.tensor_copy(y_sb[:, h, :], bank[6][:, 0:D]).then_inc(f_ye, 1)

            steps = [0]

            def link(ins):
                steps[0] += 1
                ins.then_inc(r_ch, 1)
                dve.wait_ge(r_ch, steps[0])

            dve.wait_ge(a_vev, NT)
            dve.wait_ge(s_mem, 7)
            V = nc.vector
            full = [P, NT, E, E]
            pre = bank[7][:, 0:NT * E].rearrange("p (t e) -> p t e", e=E)
            tot = bank[7][:, NT * E:2 * NT * E].rearrange("p (t e) -> p t e", e=E)
            c_end, x_end = 0, 1
            gt4 = r_gt[:, :].rearrange("p (t e f) -> p t e f", e=E, f=E)
            eq4 = r_eq[:, :].rearrange("p (t e f) -> p t e f", e=E, f=E)
            l_f = lg[:, :, :].unsqueeze(2).to_broadcast(full)
            l_e = lg[:, :, :].unsqueeze(3).to_broadcast(full)
            def route_rank():
                link(V.tensor_tensor(gt4, l_f, l_e, ALU.is_gt))
                link(V.tensor_tensor(eq4, l_f, l_e, ALU.is_equal))
                link(V.tensor_tensor(eq4, eq4, tie.unsqueeze(1).to_broadcast(full), ALU.mult))

            def route_rank2():
                link(V.tensor_tensor(r_gt[:, :], r_gt[:, :], r_eq[:, :], ALU.add))
                link(V.tensor_reduce(rank[:, :, :], gt4, AX.X, ALU.add))

            def route_select():
                for s in range(2):
                    link(V.tensor_scalar(sel[:, s, :, :], rank[:, :, :], float(s), None, ALU.is_equal))
                    link(V.tensor_tensor(tmp[:, :, :], sel[:, s, :, :], lg[:, :, :], ALU.mult))
                    link(V.tensor_reduce(best[:, s, :], tmp[:, :, :], AX.X, ALU.add))
                V.tensor_tensor(sel[:, 2, :, :], sel[:, 0, :, :], sel[:, 1, :, :], ALU.add).then_inc(r_sel, 1)
                V.tensor_tensor(wts[:, 0, :], best[:, 1, :], best[:, 0, :], ALU.subtract).then_inc(r_d, 1)

            def route_weights():
                dve.wait_ge(r_e, 1)
                link(V.tensor_scalar(wts[:, 3, :], wts[:, 1, :], 1.0, None, ALU.add))
                link(V.reciprocal(wts[:, 2, :], wts[:, 3, :]))
                link(V.tensor_tensor(wts[:, 3, :], wts[:, 1, :], wts[:, 2, :], ALU.mult))

            def route_counts():
                dve.wait_ge(r_cnt, 1)
                link(V.tensor_copy(tmp[:, :, :], tot))
                link(V.tensor_copy(cum[:, 0, 8:, :], tmp[:, :, :]))
                src = 0
                for sh in (1, 2, 4, 8):
                    link(V.tensor_tensor(cum[:, 1 - src, 8:, :], cum[:, src, 8:, :], cum[:, src, 8 - sh:8 + NT - sh, :], ALU.add))
                    src = 1 - src

            def route_tiles():
                thr = cst[:, C_THR:C_THR + NT].unsqueeze(1).to_broadcast([P, E, NT])
                cmp = r_gt[:, 0:E * NT].rearrange("p (e k) -> p e k", e=E)
                cnt = cum[:, c_end, 8 + NT - 1, :].unsqueeze(2).to_broadcast([P, E, NT])
                link(V.tensor_tensor(cmp, cnt, thr, ALU.is_gt))
                link(V.tensor_reduce(ntl[:, :], cmp, AX.X, ALU.add))
                link(V.tensor_copy(cumt[:, 0, 4:], ntl[:, :]))
                s2 = 0
                for sh in (1, 2, 4):
                    link(V.tensor_tensor(cumt[:, 1 - s2, 4:], cumt[:, s2, 4:], cumt[:, s2, 4 - sh:4 + E - sh], ALU.add))
                    s2 = 1 - s2

            def route_experts():
                cm2 = r_eq[:, 0:XTILES * E].rearrange("p (k e) -> p k e", e=E)
                link(V.tensor_tensor(cm2, cumt[:, x_end, 4:].unsqueeze(1).to_broadcast([P, XTILES, E]),
                                     cst[:, C_TIX:C_TIX + XTILES].unsqueeze(2).to_broadcast([P, XTILES, E]), ALU.is_le))
                link(V.tensor_reduce(etf[:, :], cm2, AX.X, ALU.add))
                link(V.tensor_scalar(etf[:, :], etf[:, :], float(E - 1), None, ALU.min))
                eq = r_eq[:, 0:XTILES]
                link(V.tensor_scalar(eq, etf[:, :], float(RING), -float(RING), ALU.is_ge, ALU.mult))
                V.tensor_tensor(eslot[:, :], etf[:, :], eq, ALU.add).then_inc(r_tab, 1)
                V.tensor_scalar(eready[:, :], etf[:, :], 1.0, None, ALU.add).then_inc(r_tab, 1)
                V.tensor_scalar(efree[:, :], cumt[:, x_end, 4:4 + E - RING], float(NT), None, ALU.add).then_inc(r_tab, 1)

            def route_slots():
                link(V.tensor_tensor(ntl[:, :], cumt[:, x_end, 4:], ntl[:, :], ALU.subtract))
                link(V.tensor_scalar(ntl[:, :], ntl[:, :], float(P), float(TOK), ALU.mult, ALU.add))
                link(V.tensor_tensor(slotf[:, :, :], cum[:, c_end, 8:, :], tmp[:, :, :], ALU.subtract))
                link(V.tensor_tensor(slotf[:, :, :], slotf[:, :, :], pre, ALU.add))
                link(V.tensor_tensor(slotf[:, :, :], slotf[:, :, :], ntl[:, :].unsqueeze(1).to_broadcast([P, NT, E]), ALU.add))

            def route_positions():
                for s in range(2):
                    link(V.tensor_tensor(tmp[:, :, :], sel[:, s, :, :], slotf[:, :, :], ALU.mult))
                    link(V.tensor_reduce(posf[:, s, :], tmp[:, :, :], AX.X, ALU.add))
                    V.tensor_copy(pos[:, s, :], posf[:, s, :]).then_inc(r_pos, 1)

            between = [route_rank, route_rank2, route_select, route_counts, route_tiles, route_slots, route_positions,
                       route_experts]
            between.append(lambda: None)
            low_xT(0, 0)
            for n, part in enumerate(between):
                gate_silu(n, n % 2)
                if n:
                    low_hT(n - 1, (n - 1) % 2)
                gate_up(n, n % 2)
                low_xT(n + 1, (n + 1) % 2)
                if n:
                    dve.wait_ge(f_ys[(n - 1) % 2], (n - 1) // 2 * 16 + 16)
                    ev_y(n - 1, (n - 1) % 2)
                part()
            n0 = len(between)
            with dve.Fori(0, (NF - TAIL - n0) // 2) as i:
                for h in range(2):
                    n = i * 2 + (n0 + h)
                    gate_silu(n, (n0 + h) % 2)
                    low_hT(n - 1, (n0 + h - 1) % 2)
                    gate_up(n, (n0 + h) % 2)
                    low_xT(n + 1, (n0 + h - 1) % 2)
                    dve.wait_ge(f_ys[(n0 + h - 1) % 2], i * 16 + ((n0 + h - 1) // 2 * 16 + 16))
                    ev_y(n - 1, (n0 + h - 1) % 2)

            def reduce(it, lu, j):
                dve.wait_ge(t_p1, at(it, lu + 2, 16, j + 1))
                V.tensor_reduce(mpart[:, lu % 2, j:j + 1], ps_misc if it is None else bank[FILL_BANK[j % 8]], AX.X, ALU.max).then_inc(t_red, 1)

            def negmax(it, lu):
                dve.wait_ge(t_red, at(it, lu + 2, 16, 16))
                V.tensor_reduce(q_nat[:, (lu + 2) % 4, :, :].rearrange("p t (e c) -> p t e c", e=2)[:, :, :, MCOL].bitcast(F32R),
                                mpart[:, lu % 2, :].rearrange("p (t e k) -> p t e k", e=2, k=2),
                                AX.X, ALU.max, negate=True).then_inc(t_negm, 1)

            def invert(it, lu, c):
                if c == 0:
                    dve.wait_ge(t_miscev, misc_index(it, lu, "DEN") + 1)
                    dve.wait_ge(t_nrm, at(it, lu, 1, 3))
                V.reciprocal(rden[:, c * P:(c + 1) * P], den[:, c * P:(c + 1) * P]).then_inc(t_rd, 1)

            def normalise(it, lu):
                dve.wait_ge(t_rd, at(it, lu, 4, 2))
                dve.wait_ge(t_cev, min(lu, UNITS) + 1 if it is None else at(it, lu, 1, 1))
                dve.wait_ge(t_cst[lu % 2], 16 * (lu // 2) + 16 if it is None else it * 64 + (16 * (lu // 2) + 16))
                V.tensor_tensor(ctx_nrm[:, lu % 2, :], ctx_raw[:, lu % 2, :], rden, ALU.mult).then_inc(t_nrm, 1)

            def total(it, lu):
                dve.wait_ge(t_add, at(it, lu, 6, 6))
                a = acc[:, (lu - 1) % 2, :, :, :]
                V.tensor_tensor(a[:, 0, :, :], a[:, 0, :, :], a[:, 1, :, :], ALU.add).then_inc(t_sum, 1)

            def dve_gap(n, gap):
                item, _ = gaps.get((n, gap), ((0, ""), None))
                if not isinstance(item[1], str):
                    reduce(None, *item)
                    if item[1] == 15:
                        negmax(None, item[0])

            for n in range(NF - TAIL, NF):
                dve_gap(n, 0)
                gate_silu(n, n % 2)
                low_hT(n - 1, (n - 1) % 2)
                gate_up(n, n % 2)
                dve_gap(n, 1)
                if n + 1 < NF:
                    low_xT(n + 1, (n + 1) % 2)
                dve.wait_ge(f_ys[(n - 1) % 2], (n - 1) // 2 * 16 + 16)
                ev_y(n - 1, (n - 1) % 2)
                dve_gap(n, 2)
            low_hT(NF - 1, (NF - 1) % 2)
            dve.wait_ge(f_ys[(NF - 1) % 2], (NF - 1) // 2 * 16 + 16)
            ev_y(NF - 1, (NF - 1) % 2)
            dve.wait_ge(t_set, 6)
            with dve.Fori(0, UNITS // 8) as it:
                for lu in range(8):
                    for m in range(4):
                        for j in range(4 * m, 4 * m + 4):
                            reduce(it, lu, j)
                        if m == 0:
                            invert(it, lu, 2)
                            invert(it, lu, 3)
                        if m == 1:
                            total(it, lu)
                        if m == 2:
                            normalise(it, lu)
                        if m == 3:
                            negmax(it, lu)
                            invert(it, lu, 0)
                            invert(it, lu, 1)

            f = [0]

            def olink(ins):
                f[0] += 1
                ins.then_inc(o_f, 1)
                dve.wait_ge(o_f, f[0])

            dve.wait_ge(o_w, 16)
            V.tensor_copy(wo_hi, wo).then_inc(o_whi, 1)
            dve.wait_ge(o_whi, 1)
            dve.wait_ge(o_pick, 16 + 16 * (UNITS // 8))
            V.tensor_tensor(wo_lo, wo, wo_hi.bitcast(F32), ALU.subtract).then_inc(o_wlo, 1)
            invert(None, UNITS, 2)
            invert(None, UNITS, 3)
            total(None, UNITS)
            normalise(None, UNITS)
            route_weights()
            dve.wait_ge(s_bias, 16)
            for t in range(NT):
                h = t % 2
                if t == LATE:
                    for c in range(4):
                        invert(None, UNITS if c < 2 else UNITS + 1, c)
                    normalise(None, UNITS + 1)
                dve.wait_ge(o_in[h], 32 * (t // 2 + 1))
                olink(V.tensor_tensor(fa[:, h, :], fx[:, h, :], fy[:, h, :], ALU.add))
                olink(V.tensor_tensor(fa[:, h, :], fa[:, h, :], bias[:, :], ALU.add))
                olink(V.scalar_tensor_tensor(fa[:, h, :], y_pick[:, t, 0, :], wts[:, 2, t:t + 1], fa[:, h, :], ALU.mult, ALU.add))
                olink(V.scalar_tensor_tensor(fa[:, h, :], y_pick[:, t, 1, :], wts[:, 3, t:t + 1], fa[:, h, :], ALU.mult, ALU.add))
                dve.wait_ge(o_mm, t + 1)
                dve.wait_ge(o_st[h], 16 * (t // 2 + 1))
                V.tensor_tensor(fb[:, h, :], fa[:, h, :], bank[h][:, 0:D], ALU.add).then_inc(o_done, 1)

        @block.tensor
        def _(pe):
            mm = nc.tensor.matmul
            tr = nc.tensor.transpose
            pe.wait_ge(s_cst, 16)

            def a_xT_in(t, j):
                h = j % 2
                pe.wait_ge(a_xl, t + 1)
                for k in range(KC):
                    last = tr(bank[5 * h][:, k * P:(k + 1) * P], xt4[:, j, k * P:(k + 1) * P], ident)
                last.then_inc(a_xtp, 1)

            def a_project(t, h):
                pe.wait_ge(a_xt, t + 1)
                pe.wait_ge(a_ro, t + 1)
                for k in range(KC):
                    last = mm(bank[1 + h][:, 0:QK_COLS], xT[:, h, k * P:(k + 1) * P], w_in[:, k, 0:QK_COLS],
                              start=k == 0, stop=k == KC - 1)
                last.then_inc(a_qk, 1)
                for k in range(KC):
                    last = mm(bank[3 + h][:, 0:VG_COLS], xT[:, h, k * P:(k + 1) * P], w_in[:, k, QK_COLS:],
                              start=k == 0, stop=k == KC - 1)
                last.then_inc(a_vg, 1)

            a_xT_in(0, 0)
            pe.wait_ge(s_win, 32)
            with pe.Fori(0, NT // 4 - 1) as i:
                for j in range(4):
                    a_xT_in(i * 4 + (j + 1), (j + 1) % 4)
                    a_project(i * 4 + j, j % 2)
            for t in range(NT - 4, NT):
                if t + 1 < NT:
                    a_xT_in(t + 1, (t + 1) % 4)
                a_project(t, t % 2)


            def x_T(n, h, l):
                if l is None:
                    pe.wait_ge(a_xl, NT + n + 1)
                else:
                    pe.wait_ge(f_xl[h], l)
                if not (isinstance(n, int) and n == 0):
                    pe.wait_ge(f_xt, n)
                    pe.wait_ge(f_xtl, n)
                for k in range(KC):
                    last = tr(bank[0][:, k * P:(k + 1) * P], xt_in[:, h, k * P:(k + 1) * P], ident)
                last.then_inc(f_xtp, 1)

            BASE = None

            def up(n, h, half, e):
                pe.wait_ge(f_xt, n + 1)
                pe.wait_ge(f_xtl, n + 1)
                for k in range(KC):
                    o = k * 2 * I + half * I
                    if e is BASE:
                        hi, lo = base_gu_w[:, o:o + I], base_gu_w[:, GU + o:GU + o + I]
                    else:
                        hi, lo = ring[:, ds(e * (2 * WS) + o, I)], ring[:, ds(e * (2 * WS) + (WS + o), I)]
                    x_hi, x_lo = xT_hi[:, h, k * P:(k + 1) * P], xT_lo[:, h, k * P:(k + 1) * P]
                    for j, (a, b) in enumerate([(x_hi, hi), (x_hi, lo), (x_lo, hi)]):
                        last = mm(bank[1 + 2 * h + half], a, b,
                                  start=k == 0 and j == 0, stop=k == KC - 1 and j == 2)
                last.then_inc((f_g, f_u)[half], 1)

            def h_T(n, h):
                pe.wait_ge(f_h, n + 1)
                for k in range(IC):
                    last = tr(bank[5][:, k * P:(k + 1) * P], hid[:, h, k * P:(k + 1) * P], ident)
                last.then_inc(f_htp, 1)

            def down(n, h, e):
                pe.wait_ge(f_ht, n + 1)
                pe.wait_ge(f_htl, n + 1)
                for k in range(IC):
                    o = k * D
                    if e is BASE:
                        hi, lo = base_dn_w[:, o:o + D], base_dn_w[:, DN + o:DN + o + D]
                    else:
                        hi, lo = ring[:, ds(e * (2 * WS) + (GU + o), D)], ring[:, ds(e * (2 * WS) + (WS + GU + o), D)]
                    h_hi, h_lo = hidT_hi[:, h, k * P:(k + 1) * P], hidT_lo[:, h, k * P:(k + 1) * P]
                    for j, (a, b) in enumerate([(h_hi, hi), (h_hi, lo), (h_lo, hi)]):
                        last = mm(bank[6][:, 0:D], a, b,
                                  start=k == 0 and j == 0, stop=k == IC - 1 and j == 2)
                last.then_inc(f_y, 1)

            def step(n, h, xl, e_before, e, e_next, gap=lambda g: None):
                gap(0)
                h_T(n - 1, 1 - h)
                up(n, h, 1, e)
                nxt = e_next()
                gap(1)
                if xl is not None:
                    x_T(n + 1, 1 - h, xl)
                before = e_before()
                if not (isinstance(n, int) and n == 1):
                    pe.wait_ge(f_ye, n - 1)
                down(n - 1, 1 - h, before)
                gap(2)
                if xl is not None:
                    up(n + 1, 1 - h, 0, nxt)
                return nxt

            def base():
                return BASE

            x_T(0, 0, None)
            pe.wait_ge(a_ro, NT + 2)
            pe.wait_ge(a_vev, NT)
            pe.wait_ge(b_split, 3)
            up(0, 0, 0, BASE)
            up(0, 0, 1, BASE)
            x_T(1, 1, None)
            up(1, 1, 0, BASE)
            for n in range(1, 4):
                step(n, n % 2, 16 * ((n + 1) // 2), base, BASE, base)
            pe.wait_ge(r_sel, 1)
            pe.wait_ge(s_mem, 2)
            sflat = sel[:, 2, :, :].rearrange("p t e -> p (t e)")
            mm(bank[7][:, 0:NT * E], tri, sflat, start=True, stop=True)
            mm(bank[7][:, NT * E:2 * NT * E], ones[:, :], sflat, start=True, stop=True).then_inc(r_cnt, 1)
            step(4, 0, 32, base, BASE, base)
            with pe.Fori(0, (NT - 6) // 2) as i:
                for h in range(2):
                    step(i * 2 + (5 + h), 1 - h, i * 16 + 48, base, BASE, base)
            pe.wait_ge(r_tab, 3)

            def slot_of(k):
                slot = pe.value_load(eslot[0:1, k:k + 1] if isinstance(k, int) else eslot[0:1, ds(k, 1)])
                return slot.with_bounds(min_val=0, max_val=RING - 1)

            e0 = step(NT - 1, 1, 16 * (NT // 2), base, BASE, lambda: slot_of(0))
            step(NT, 0, 16 * (NT // 2), base, e0, lambda: slot_of(1))
            with pe.Fori(0, (NF - TAIL - NT - 1) // 2) as i:
                e0 = slot_of(i * 2 + 1)
                e1 = step(i * 2 + (NT + 1), 1, i * 16 + 16 * (NT // 2 + 1),
                          lambda: slot_of(i * 2), e0, lambda: slot_of(i * 2 + 2))
                step(i * 2 + (NT + 2), 0, i * 16 + 16 * (NT // 2 + 1), lambda: e0, e1, lambda: slot_of(i * 2 + 3))

            def misc(it, lu, name):
                pe.wait_ge(t_miscev, misc_index(it, lu, name)) if not (it is None and (lu, name) == PRO[0]) else None
                if it is not None:
                    pe.wait_ge(t_red, at(it, lu + 2, 16, 4 * ((SLOT[name] + 1) // 2) - 1))
                if name == "T1":
                    v = lu + 3
                    cnt = v // 4 * 16 + 16 if it is None else it * 32 + (v // 4 * 16 + 16)
                    pe.wait_ge(t_q[v % 4], cnt)
                    for j in range(QT):
                        last = tr(ps_misc[:, j * P:(j + 1) * P], q_nat[:, v % 4, j, :], ident)
                elif name == "T2":
                    v = lu + 1
                    pe.wait_ge(t_negm, at(it, v, 1, 1))
                    for j in range(QT):
                        last = tr(ps_misc[:, j * P:(j + 1) * P], q_nat[:, v % 4, j, :], ident)
                elif name == "DEN":
                    pe.wait_ge(t_sum, at(it, lu, 1, 1))
                    for e in range(2):
                        last = mm(ps_misc[e * DV:(e + 1) * DV, :], ones[:, 0:DV], acc[:, (lu - 1) % 2, 0, e, :],
                                  start=True, stop=True)
                else:
                    k = int(name[1])
                    g1 = 16 if it is None else it * 32 + (lu // 4 * 16 + 32)
                    pe.wait_ge(t_k, g1)
                    var = k // 2
                    c0 = ST * (1 - var)
                    for j in range(QT):
                        last = tr(ps_misc[:, j * P:(j + 1) * P], k_nat[:, (k % 2) * QT + j, c0:c0 + P], ident)
                last.then_inc(t_misc, 1)

            def fill(it, lu, j):
                qt, e, kc = j // 4, j // 2 % 2, j % 2
                if it is not None:
                    pe.wait_ge(t_red, at(it, lu + 2, 16, j - FILL_AGO[j % 8] + 1))
                    if j % 4 == 2:
                        pe.wait_ge(t_miscev, misc_before(it, lu, j // 4))
                if j == 0:
                    pe.wait_ge(t_miscev, before_unit(it, lu))
                g2 = (lu + 2) // 4 % 2
                mm(ps_misc if it is None else bank[FILL_BANK[j % 8]], QT1[:, lu % 2, qt * P:(qt + 1) * P], KT[:, g2, e, kc * 512:(kc + 1) * 512],
                   start=True, stop=True).then_inc(t_p1, 1)

            def scores(it, lu, kt):
                pe.wait_ge(t_e, at(it, lu, 8, kt + 1))
                if kt == 0:
                    pe.wait_ge(t_miscev, before_unit(it, lu))
                g2 = lu // 4 % 2
                for e in range(2):
                    last = mm(ps_s[kt % 2][:, e * 512:(e + 1) * 512], KT[:, g2, e, kt * P:(kt + 1) * P], QT2[:, lu % 2, :],
                              start=True, stop=True)
                last.then_inc(t_s, 1)

            def weighted(it, lu, kt, start, stop):
                g2 = lu // 4 % 2
                for e in range(2):
                    last = mm(ps_ctx[e * DV:(e + 1) * DV, :], v_nat[:, g2, kt, :], probs[:, kt, e, :], start=start, stop=stop)
                last.then_inc(t_pv, 1)

            def pe_gap(n, gap):
                item, before = gaps.get((n, gap), (None, None))
                if item is None:
                    return
                if before is not None and not isinstance(before[1], str):
                    pe.wait_ge(t_red, at(None, before[0] + 2, 16, before[1] + 1))
                elif before is not None:
                    pe.wait_ge(t_miscev, misc_index(None, *before) + 1)
                if isinstance(item[1], str):
                    misc(None, *item)
                else:
                    fill(None, *item)

            pe.wait_ge(t_kpad, 2)
            e0, e1 = slot_of(NF - TAIL - NT - 1), slot_of(NF - TAIL - NT)
            for n in range(NF - TAIL, NF):
                more = n + 1 < NF
                e2 = step(n, n % 2, 16 * ((n + 1) // 2) if more else None, lambda: e0, e1,
                          (lambda: slot_of(n + 1 - NT)) if more else base, gap=lambda g: pe_gap(n, g))
                e0, e1 = e1, e2
            h_T(NF - 1, (NF - 1) % 2)
            pe.wait_ge(f_ye, NF - 1)
            down(NF - 1, (NF - 1) % 2, e0)

            pe.wait_ge(f_ye, NF)
            pe.wait_ge(t_set, 6)
            pe.wait_ge(t_red, 32)
            weighted(None, -1, 7, True, False)
            with pe.Fori(0, UNITS // 8) as it:
                for lu in range(8):
                    for m in range(4):
                        fill(it, lu, 4 * m)
                        fill(it, lu, 4 * m + 1)
                        for name in misc_of(lu, 2 * m):
                            misc(it, lu, name)
                        scores(it, lu, 2 * m)
                        scores(it, lu, 2 * m + 1)
                        fill(it, lu, 4 * m + 2)
                        fill(it, lu, 4 * m + 3)
                        if m == 0:
                            pe.wait_ge(t_e, at(it, lu, 8, 2))
                            weighted(it, lu - 1, 6, False, False)
                            weighted(it, lu - 1, 7, False, True)
                        else:
                            pe.wait_ge(t_e, at(it, lu, 8, 2 * m + 2))
                            if m == 1:
                                pe.wait_ge(t_cev, at(it, lu, 1, 1))
                                pe.wait_ge(t_v[lu // 4 % 2], it * 16 + 16)
                            weighted(it, lu, 2 * m - 2, m == 1, False)
                            weighted(it, lu, 2 * m - 1, False, False)
                        for name in misc_of(lu, 2 * m + 1):
                            misc(it, lu, name)
            pe.wait_ge(t_e, 8 * UNITS + 2)
            weighted(None, UNITS - 1, 6, False, False)
            weighted(None, UNITS - 1, 7, False, True)
            pe.wait_ge(o_wlo, 1)
            for t in range(NT):
                h = t % 2
                if t == LATE:
                    pe.wait_ge(t_sum, UNITS + 1)
                    pe.wait_ge(t_miscev, len(PRO) + 4 * len(BODY))
                    pe.wait_ge(t_red, 16 * (UNITS + 2))
                    for e in range(2):
                        last = mm(ps_misc[e * DV:(e + 1) * DV, :], ones[:, 0:DV], acc[:, 1, 0, e, :], start=True, stop=True)
                    last.then_inc(t_misc, 1)
                pe.wait_ge(o_lo, t + 1)
                if t >= 2:
                    pe.wait_ge(o_done, t - 1)
                for c in range(PAIRS):
                    for j, (a, b) in enumerate([(ct_hi, wo_hi), (ct_hi, wo_lo), (ct_lo, wo_hi)]):
                        last = mm(bank[h][:, 0:D], a[:, t % 4, c, :], b[:, c, :],
                                  start=c == 0 and j == 0, stop=c == PAIRS - 1 and j == 2)
                last.then_inc(o_mm, 1)
    return nc


def make_consts():
    import numpy as np
    c = np.zeros((P, C_ALL), np.float32)
    c[:, C_ID:C_ID + P] = np.eye(P)
    c[:, C_TRI:C_TRI + P] = np.triu(np.ones((P, P)), 1)
    inv = (1.0 / np.float32(10000.0) ** (np.arange(0, DK, 2, dtype=np.float32) / np.float32(DK))).astype(np.float32)
    ang = np.arange(L, dtype=np.float32)[:, None] * inv[None, :]
    sin, cos = np.sin(ang).astype(np.float32), np.cos(ang).astype(np.float32)

    def tiles(a):
        return a.reshape(TB, P, DK).transpose(1, 0, 2).reshape(P, TB * DK)

    c[:, C_COS:C_COS + TB * DK] = tiles(np.concatenate([cos, cos], 1))
    c[:, C_SIN:C_SIN + TB * DK] = tiles(np.concatenate([-sin, sin], 1))
    c[:, C_TIE:C_TIE + E * E] = (np.arange(E)[None, :] < np.arange(E)[:, None]).astype(np.float32).reshape(-1)
    c[:, C_THR:C_THR + NT] = P * np.arange(NT)
    c[:, C_THR] = -1
    c[:, C_TIX:C_TIX + XTILES] = np.arange(XTILES)
    return c


_INS = ["L0_attn_x", "L0_attn_W_attn", "L0_attn_W_out", "L0_attn_b_out", "L0_ffn_gate_w", "L0_ffn_base_gate_up",
        "L0_ffn_base_down", "L0_ffn_expert_gate_up", "L0_ffn_expert_down"]


def kernel(**inputs):
    import numpy as np
    import concourse.bacc as bacc
    from concourse.bass_utils import run_bass_kernel_spmd

    nc = bacc.Bacc("TRN2", target_bir_lowering=False, num_devices=1)
    arrays, args = {}, []
    for name in _INS:
        a = np.ascontiguousarray(inputs[name])
        arrays[name] = a
        args.append(nc.dram_tensor(name, a.shape, mybir.dt.from_np(a.dtype), kind="ExternalInput").ap())
    arrays["consts"] = make_consts()
    args.append(nc.dram_tensor("consts", arrays["consts"].shape, mybir.dt.float32, kind="ExternalInput").ap())
    args.append(nc.dram_tensor("out", (B, L, D), mybir.dt.float32, kind="ExternalOutput").ap())
    build(nc, *args)
    r = run_bass_kernel_spmd(nc, [arrays], core_ids=[0])
    return r.results[0]["out"]
```
